# Optimizing a Trainium2 kernel written in Bass

```python
import numpy as np
import jax
import jax.numpy as jnp

def _softmax(x, axis=-1):
    return jax.nn.softmax(x, axis=axis)

def _gelu(x):
    return jax.nn.gelu(x, approximate=True)

def _silu(x):
    return jax.nn.silu(x)

def _sigmoid(x):
    return jax.nn.sigmoid(x)

def _layernorm(x, axis=-1, eps=1e-05):
    m = jnp.mean(x, axis=axis, keepdims=True)
    v = jnp.var(x, axis=axis, keepdims=True)
    return (x - m) / jnp.sqrt(v + eps)

def _scatter_add(tgt, idx, src, axis=0):
    return tgt.at[idx].add(src)

def _segment_sum(src, seg, n):
    return jax.ops.segment_sum(src, seg, n)
kernel_name = 'mk_seq_postln_d1_jaxref_r8_f08679'

def setup_inputs(seed: int=0):
    np.random.seed(seed)
    _w = jnp.asarray

    def _L0_attn_setup():
        import jax, jax.numpy as jnp
        import numpy as np
        N_EMBD = 128
        N_HEAD = 16
        HEAD_DIM = N_EMBD // N_HEAD
        KV_RANK = 32
        Q_RANK = 64
        ROPE_DIM = 32
        B, T = (2, 256)
        EPS = 1e-06

        def _rope_tables(T, dim):
            inv_freq = 1.0 / 10000.0 ** (np.arange(0, dim, 2, dtype=np.float32) / dim)
            t = np.arange(T, dtype=np.float32)
            freqs = np.outer(t, inv_freq)
            emb = np.concatenate([freqs, freqs], -1)
            return (jnp.asarray(np.cos(emb)), jnp.asarray(np.sin(emb)))

        def _apply_rope(x, cos, sin):
            d2 = x.shape[-1] // 2
            x1, x2 = (x[..., :d2], x[..., d2:])
            rot = jnp.concatenate([-x2, x1], axis=-1)
            return x * cos[None, None, :, :] + rot * sin[None, None, :, :]
        key = jax.random.key(seed)
        ks = jax.random.split(key, 10)

        def w(k, fan_in, fan_out):
            return jax.random.normal(k, (fan_in, fan_out), dtype=jnp.float32) * fan_in ** (-0.5)
        return {'x': jax.random.normal(ks[0], (B, T, N_EMBD), dtype=jnp.float32), 'W_kv': w(ks[1], N_EMBD, KV_RANK), 'g_kv': jnp.ones((KV_RANK,), dtype=jnp.float32), 'W_kdec': w(ks[2], KV_RANK, N_HEAD * HEAD_DIM), 'W_vdec': w(ks[3], KV_RANK, N_HEAD * HEAD_DIM), 'W_q': w(ks[4], N_EMBD, Q_RANK), 'W_qdec': w(ks[5], Q_RANK, N_HEAD * HEAD_DIM), 'W_krope': w(ks[6], N_EMBD, N_HEAD * ROPE_DIM), 'W_qrope': w(ks[7], Q_RANK, N_HEAD * ROPE_DIM), 'W_o': w(ks[8], N_HEAD * HEAD_DIM, N_EMBD)}
    _L0_attn_in = _L0_attn_setup()

    def _L0_ffn_setup():
        import jax, jax.numpy as jnp
        import numpy as np
        E = 16
        G = 4
        EPG = E // G
        K = 4
        TOPK_GROUP = 2
        PER_GROUP_K = K // TOPK_GROUP

        def _route(xf, router_w, correction_bias):
            S = xf.shape[0]
            logits = xf @ router_w.T
            scores = jax.nn.sigmoid(logits)
            sb = scores + correction_bias
            grp_top = jax.lax.top_k(sb.reshape(S, G, EPG), PER_GROUP_K)[0]
            group_scores = grp_top.sum(axis=-1)
            _, group_idx = jax.lax.top_k(group_scores, TOPK_GROUP)
            group_mask = jnp.zeros((S, G), sb.dtype).at[jnp.arange(S)[:, None], group_idx].set(1.0)
            score_mask = jnp.broadcast_to(group_mask[:, :, None], (S, G, EPG)).reshape(S, E)
            masked = jnp.where(score_mask > 0, sb, -jnp.inf)
            _, topk_idx = jax.lax.top_k(masked, K)
            w = jnp.take_along_axis(scores, topk_idx, axis=1)
            w = w / (w.sum(axis=-1, keepdims=True) + 1e-20)
            return (topk_idx, w, scores)
        key = jax.random.key(seed)
        ks = jax.random.split(key, 9)
        B, T, C, H, HS = (2, 128, 128, 32, 256)
        std = 0.02
        return {'x': jax.random.normal(ks[0], (B, T, C), jnp.float32), 'router_w': jax.random.normal(ks[1], (E, C), jnp.float32) * std, 'correction_bias': jnp.zeros((E,), jnp.float32), 'gate_w': jax.random.normal(ks[2], (E, C, H), jnp.float32) * std, 'up_w': jax.random.normal(ks[3], (E, C, H), jnp.float32) * std, 'down_w': jax.random.normal(ks[4], (E, H, C), jnp.float32) * std, 'shared_gate_w': jax.random.normal(ks[5], (HS, C), jnp.float32) * std, 'shared_up_w': jax.random.normal(ks[6], (HS, C), jnp.float32) * std, 'shared_down_w': jax.random.normal(ks[7], (C, HS), jnp.float32) * std}
    _L0_ffn_in = _L0_ffn_setup()
    _d = {'L0_attn_x': _L0_attn_in['x'], 'L0_attn_W_kv': _L0_attn_in['W_kv'], 'L0_attn_g_kv': _L0_attn_in['g_kv'], 'L0_attn_W_kdec': _L0_attn_in['W_kdec'], 'L0_attn_W_vdec': _L0_attn_in['W_vdec'], 'L0_attn_W_q': _L0_attn_in['W_q'], 'L0_attn_W_qdec': _L0_attn_in['W_qdec'], 'L0_attn_W_krope': _L0_attn_in['W_krope'], 'L0_attn_W_qrope': _L0_attn_in['W_qrope'], 'L0_attn_W_o': _L0_attn_in['W_o'], 'L0_ffn_router_w': _L0_ffn_in['router_w'], 'L0_ffn_correction_bias': _L0_ffn_in['correction_bias'], 'L0_ffn_gate_w': _L0_ffn_in['gate_w'], 'L0_ffn_up_w': _L0_ffn_in['up_w'], 'L0_ffn_down_w': _L0_ffn_in['down_w'], 'L0_ffn_shared_gate_w': _L0_ffn_in['shared_gate_w'], 'L0_ffn_shared_up_w': _L0_ffn_in['shared_up_w'], 'L0_ffn_shared_down_w': _L0_ffn_in['shared_down_w']}
    _x0 = _d['L0_attn_x']
    _d['L0_attn_x'] = jax.random.normal(jax.random.fold_in(jax.random.key(seed), 1), (16, 512, 128), dtype=_x0.dtype)
    del _x0
    return _d

def reference(L0_attn_x, L0_attn_W_kv, L0_attn_g_kv, L0_attn_W_kdec, L0_attn_W_vdec, L0_attn_W_q, L0_attn_W_qdec, L0_attn_W_krope, L0_attn_W_qrope, L0_attn_W_o, L0_ffn_router_w, L0_ffn_correction_bias, L0_ffn_gate_w, L0_ffn_up_w, L0_ffn_down_w, L0_ffn_shared_gate_w, L0_ffn_shared_up_w, L0_ffn_shared_down_w):

    def _L0_attn_ref(x, W_kv, g_kv, W_kdec, W_vdec, W_q, W_qdec, W_krope, W_qrope, W_o):
        import jax, jax.numpy as jnp
        import numpy as np
        N_EMBD = 128
        N_HEAD = 16
        HEAD_DIM = N_EMBD // N_HEAD
        KV_RANK = 32
        Q_RANK = 64
        ROPE_DIM = 32
        B, T = (2, 256)
        EPS = 1e-06

        def _rope_tables(T, dim):
            inv_freq = 1.0 / 10000.0 ** (np.arange(0, dim, 2, dtype=np.float32) / dim)
            t = np.arange(T, dtype=np.float32)
            freqs = np.outer(t, inv_freq)
            emb = np.concatenate([freqs, freqs], -1)
            return (jnp.asarray(np.cos(emb)), jnp.asarray(np.sin(emb)))

        def _apply_rope(x, cos, sin):
            d2 = x.shape[-1] // 2
            x1, x2 = (x[..., :d2], x[..., d2:])
            rot = jnp.concatenate([-x2, x1], axis=-1)
            return x * cos[None, None, :, :] + rot * sin[None, None, :, :]
        Bx, Tx, C = x.shape
        kv_c = x @ W_kv
        kv_c = kv_c * jax.lax.rsqrt(jnp.mean(kv_c * kv_c, axis=-1, keepdims=True) + EPS) * g_kv
        q_c = x @ W_q

        def heads(y, d):
            return y.reshape(Bx, Tx, N_HEAD, d).transpose(0, 2, 1, 3)
        k_content = heads(kv_c @ W_kdec, HEAD_DIM)
        v = heads(kv_c @ W_vdec, HEAD_DIM)
        q_content = heads(q_c @ W_qdec, HEAD_DIM)
        k_rope = heads(x @ W_krope, ROPE_DIM)
        q_rope = heads(q_c @ W_qrope, ROPE_DIM)
        cos, sin = _rope_tables(Tx, ROPE_DIM)
        q_rope = _apply_rope(q_rope, cos, sin)
        k_rope = _apply_rope(k_rope, cos, sin)
        q = jnp.concatenate([q_content, q_rope], axis=-1)
        k = jnp.concatenate([k_content, k_rope], axis=-1)
        scale = 1.0 / jnp.sqrt(jnp.float32(q.shape[-1]))
        scores = jnp.einsum('bhqd,bhkd->bhqk', q, k) * scale
        causal = jnp.tril(jnp.ones((Tx, Tx), dtype=bool))
        scores = jnp.where(causal[None, None], scores, jnp.float32(-jnp.inf))
        attn = jax.nn.softmax(scores, axis=-1)
        out = jnp.einsum('bhqk,bhkd->bhqd', attn, v)
        out = out.transpose(0, 2, 1, 3).reshape(Bx, Tx, N_HEAD * HEAD_DIM)
        return out @ W_o

    def _L0_ffn_ref(x, router_w, correction_bias, gate_w, up_w, down_w, shared_gate_w, shared_up_w, shared_down_w):
        import jax, jax.numpy as jnp
        import numpy as np
        E = 16
        G = 4
        EPG = E // G
        K = 4
        TOPK_GROUP = 2
        PER_GROUP_K = K // TOPK_GROUP

        def _route(xf, router_w, correction_bias):
            S = xf.shape[0]
            logits = xf @ router_w.T
            scores = jax.nn.sigmoid(logits)
            sb = scores + correction_bias
            grp_top = jax.lax.top_k(sb.reshape(S, G, EPG), PER_GROUP_K)[0]
            group_scores = grp_top.sum(axis=-1)
            _, group_idx = jax.lax.top_k(group_scores, TOPK_GROUP)
            group_mask = jnp.zeros((S, G), sb.dtype).at[jnp.arange(S)[:, None], group_idx].set(1.0)
            score_mask = jnp.broadcast_to(group_mask[:, :, None], (S, G, EPG)).reshape(S, E)
            masked = jnp.where(score_mask > 0, sb, -jnp.inf)
            _, topk_idx = jax.lax.top_k(masked, K)
            w = jnp.take_along_axis(scores, topk_idx, axis=1)
            w = w / (w.sum(axis=-1, keepdims=True) + 1e-20)
            return (topk_idx, w, scores)
        B, T, C = x.shape
        S = B * T
        xf = x.reshape(S, C)
        sg = xf @ shared_gate_w.T
        su = xf @ shared_up_w.T
        shared_out = jax.nn.silu(sg) * su @ shared_down_w.T
        topk_idx, w, _scores = _route(xf, router_w, correction_bias)
        combine = jnp.zeros((S, E), xf.dtype).at[jnp.arange(S)[:, None], topk_idx].add(w)
        g = jnp.einsum('sc,ech->esh', xf, gate_w)
        u = jnp.einsum('sc,ech->esh', xf, up_w)
        h = jax.nn.silu(g) * u
        hw = h * combine.T[:, :, None]
        routed = jnp.einsum('esh,ehc->sc', hw, down_w)
        return (shared_out + routed).reshape(B, T, C)
    x = L0_attn_x
    x = _layernorm(x + _L0_attn_ref(x, L0_attn_W_kv, L0_attn_g_kv, L0_attn_W_kdec, L0_attn_W_vdec, L0_attn_W_q, L0_attn_W_qdec, L0_attn_W_krope, L0_attn_W_qrope, L0_attn_W_o), axis=-1)
    x = _layernorm(x + _L0_ffn_ref(x, L0_ffn_router_w, L0_ffn_correction_bias, L0_ffn_gate_w, L0_ffn_up_w, L0_ffn_down_w, L0_ffn_shared_gate_w, L0_ffn_shared_up_w, L0_ffn_shared_down_w), axis=-1)
    return x

_drawn_inputs = setup_inputs


def setup_inputs(seed=0):
    import zlib

    import numpy as np

    out = dict(_drawn_inputs(seed))
    spreads = {'L0_attn_g_kv': (1.0, 0.2), 'L0_ffn_correction_bias': (0.0, 0.8)}
    factors = {'L0_ffn_router_w': 8.0,
     'L0_ffn_gate_w': 8.0,
     'L0_ffn_up_w': 8.0,
     'L0_ffn_down_w': 8.0,
     'L0_ffn_shared_gate_w': 6.955,
     'L0_ffn_shared_up_w': 6.856,
     'L0_ffn_shared_down_w': 6.902}
    for name, (base, spread) in spreads.items():
        noise = np.random.default_rng([zlib.crc32(name.encode()), seed]).standard_normal(out[name].shape)
        drawn = base * np.exp(spread * noise) if base else spread * noise
        out[name] = jnp.asarray(drawn.astype(out[name].dtype))
    for name, factor in factors.items():
        out[name] = (out[name] * factor).astype(out[name].dtype)
    return out
```

```python
import concourse.bass as bass
from concourse import mybir
from contextlib import ExitStack

B, T, C = 16, 512, 128
NH, HD, RD = 16, 8, 32
FD = HD + RD
QR, KR = 64, 32
E, NG, HE = 16, 4, 32
EG = E // NG
TOPG, TOPK = 2, 4
HS = 256
P = 128
NT = T // P
RMS_EPS, LN_EPS = 1e-6, 1e-5
FB = FD * NH // P
HG = 4
GROUPS = NH // HG
PAIRS = NH // 2
SCALE = 1.0 / float(FD) ** 0.5
HIDDEN = -1e30
SLOT = 32
PS = 5
ROUTE_LINKS = 24

MAX_STEPS = (((3, 0),), ((2, 0), (0, 384)), ((1, 0),))
EXP_STEPS = (((0, 0, 0),), ((0, 1, 0), (0, 3, 384)), ((1, 0, 0),), ((1, 1, 0), (1, 3, 384)),
             ((0, 2, 0), (1, 2, 256)))


def attention_steps():
    steps = [("max", u, k) for u in (0, 1) for k in range(3)] + [("rows", 0, 0)]
    steps += [("max", 2, k) for k in range(3)]
    for u in range(PAIRS):
        ahead = u + 3
        for k in range(PS):
            if k == 2 and u % 2 == 1 and u < PAIRS - 2:
                steps.append(("rows", (u + 1) // 2, 0))
            if k == 3 and u % 2 == 0 and u:
                steps.append(("pv", u // 2 - 1, 0))
            if k in (0, 2, 4) and ahead < PAIRS:
                steps.append(("max", ahead, k // 2))
            steps.append(("exp", u, k))
        if u % 2 == 0 and u:
            steps.append(("turn", u // 2 - 1, 0))
    steps += [("pv", GROUPS - 1, 0), ("turn", GROUPS - 1, 0)]
    return steps


STEPS = attention_steps()


def pieces(h):
    first, end = FD * h, FD * h + FD
    cut = min(end, (first // P + 1) * P)
    found = [(0, cut - first, first // P, first % P)]
    if cut < end:
        found.append((cut - first, end - cut, cut // P, 0))
    return found


STACK_DMAS = [6 * sum(len(pieces(h)) for h in range(HG * g, HG * g + HG)) for g in range(GROUPS)]


def mla_moe_kernel(nc, x, w_qkv, w_kvdec, g_kv, w_qdec, w_krope, w_qrope, w_o, router, bias,
                   gate, up, down, sgate, sup, sdown, cos, sin, out, x1_dram, x1t_dram, cw_dram):
    f32, f32r, bf16 = mybir.dt.float32, mybir.dt.float32r, mybir.dt.bfloat16
    ALU, ACT, AX = mybir.AluOpType, mybir.ActivationFunctionType, mybir.AxisListType
    ctx = ExitStack()

    def sb(name, shape, dt=f32):
        return ctx.enter_context(nc.sbuf_tensor(name, shape, dt))

    def sem(name):
        return ctx.enter_context(nc.semaphore(name))

    with ctx:
        wqkv = sb("wqkv", [P, QR + KR])
        wkvd = sb("wkvd", [QR + KR, 2 * P])
        wkvg = sb("wkvg", [QR + KR, 2 * P])
        gkv = sb("gkv", [QR + KR, 1])
        ones = sb("ones", [QR + KR, 1])
        wqd = sb("wqd", [QR, P])
        wkr = sb("wkr", [P, RD * NH])
        wqr = sb("wqr", [QR, RD * NH])
        wo = sb("wo", [P, C])
        rw = sb("rw", [P, E])
        bias_sb = sb("bias_sb", [P, E])
        cos_sb = sb("cos_sb", [P, NT, RD])
        sin_sb = sb("sin_sb", [P, NT, RD])
        ident = sb("ident", [P, P])
        identb = sb("identb", [P, P], bf16)
        maskb = sb("maskb", [P, P], bf16)
        lower = sb("lower", [P, E, E])
        mhalf = sb("mhalf", [P, NT])
        tick = sb("tick", [P, 2])
        xn = sb("xn", [P, NT, C])
        xr = sb("xr", [P, NT, C])
        xt = sb("xt", [P, T])
        qct = sb("qct", [QR + KR, T])
        sq = sb("sq", [QR + KR, T])
        ms = sb("ms", [P, NT])
        rr = sb("rr", [P, NT])
        feat = [sb("kf", [P, 2, NH, FD]), sb("qf", [P, 2, NH, FD])]
        turned = [sb("tk", [P, 2, NH, RD]), sb("tq", [P, 2, NH, RD])]
        hi = [sb("khi", [P, FB, T], f32r), sb("qhi", [P, FB, T], f32r)]
        lo = [sb("klo", [P, FB, T], f32r), sb("qlo", [P, FB, T], f32r)]
        ks = sb("ks", [P, NH, T], f32r)
        qs = sb("qs", [P, NH, T], f32r)
        va = sb("va", [P, NT, NH, SLOT])
        probs = sb("probs", [P, 2, 2 * PS, T])
        nm = sb("nm", [P, 2, NT, HG])
        rows = sb("rows", [HG, 1, 2, T], f32r)
        ot = sb("ot", [P, 2, T])
        rs = sb("rs", [P, NT, HG])
        on = sb("on", [P, NT, NH, HD])
        st6 = sb("st6", [P, NT, 6])
        mv = sb("mv", [P, NT, 2])
        ve = sb("ve", [P, NT])
        rstd = sb("rstd", [P, NT])
        x1 = sb("x1", [P, NT, C])
        x1t = sb("x1t", [P, T])
        ont = x1t
        z = xr
        sc = sb("sc", [P, NT, E])
        sbias = sb("sbias", [P, NT, E])
        t2 = sb("t2", [P, 8, NT * NG])
        gmask = sb("gmask", [P, NT, NG])
        masked = sb("masked", [P, NT, E])
        big = turned[0][:, :, :, 0:E]
        rank = sb("rank", [P, NT, E])
        cw = sb("cw", [P, NT, E])
        wsum = sb("wsum", [P, 2, NT])

        psum = ctx.enter_context(nc.psum_tensor("psum", [P, 8, T], f32))

        s_w = sem("weights_loaded")
        s_zero = sem("pool_zeroed")
        s_zeroed = sem("vector_zeroed")
        s_const = sem("constants_made")
        CONSTS = 9
        s_x = sem("x_loaded")
        s_xr = sem("residual_loaded")
        s_xtp = sem("x_transposed")
        s_xtc = sem("xt_copied")
        s_qkv = sem("latents_made")
        s_qct = sem("latents_copied")
        s_proj = sem("tile_projected")
        s_ms = sem("mean_square_ready")
        s_rr = sem("inverse_rms_ready")
        s_cont = sem("content_copied")
        s_prod = sem("rotary_products_ready")
        s_rope = sem("rotary_added")
        s_ftr = sem("features_transposed")
        s_hi = sem("high_parts_ready")
        s_lo = sem("low_parts_ready")
        s_stk = [sem(f"stacked{g}") for g in range(GROUPS)]
        s_mx = sem("max_scores_made")
        s_mxr = sem("maxima_taken")
        s_nmt = sem("maxima_transposed")
        s_mh = sem("max_hi_ready")
        s_ml = sem("max_lo_ready")
        s_row = [sem(f"max_rows_placed{g}") for g in range(GROUPS)]
        s_st = sem("scores_made")
        s_exp = sem("exponentials_ready")
        s_msk = sem("future_zeroed")
        s_pv = sem("values_weighted")
        s_oc = sem("weighted_copied")
        s_otr = sem("weighted_transposed")
        s_on = sem("heads_normalised")
        s_ont = sem("heads_transposed")
        s_ontc = sem("heads_copied")
        s_y = sem("attention_projected")
        s_var = sem("variance_ready")
        s_rstd = sem("rstd_ready")
        s_x1 = sem("x1_ready")
        s_x1tp = sem("x1_transposed")
        s_x1tc = sem("x1t_copied")
        s_lg = sem("logits_made")
        s_el = sem("logit_exponentials_ready")
        s_cw = sem("expert_weights_ready")
        s_kept = sem("x1_stored")
        s_keptt = sem("x1t_stored")
        s_keptw = sem("expert_weights_stored")
        s_dve = sem("dve_chain")

        FE = E * HE
        FH = FE + HS
        HB = FH // P
        arena = probs[:, :, :, :].rearrange("p a s t -> p (a s t)")
        taken = [0]

        def view(size):
            taken[0] += size
            return arena[:, taken[0] - size:taken[0]]

        wge, wue, wsh, wdn = view(FE), view(FE), view(2 * HS), view(FH)
        xd = [view(NT * C).rearrange("p (n d) -> p n d", n=NT) for _ in range(2)]
        xdt = [view(T) for _ in range(2)]
        cwd = [view(NT * E).rearrange("p (n e) -> p n e", n=NT) for _ in range(2)]
        act_out = [view(FH) for _ in range(2)]
        hid = [view(FH) for _ in range(2)]
        hidt = [view(FH).rearrange("p (k t) -> p k t", k=HB) for _ in range(2)]
        zd = [view(NT * C).rearrange("p (n d) -> p n d", n=NT) for _ in range(2)]
        yd = [v[:, :, :] for v in (xn, x1)]
        s_we = sem("expert_matrices_loaded")
        s_dx = [sem(f"chunk_loaded{q}") for q in range(2)]
        s_g = sem("gates_made")
        s_u = sem("hidden_made")
        s_act = sem("gates_activated")
        s_hid = sem("hidden_multiplied")
        s_hw = sem("hidden_weighted")
        s_ht = sem("hidden_transposed")
        s_hta = sem("hidden_copied_by_scalar")
        s_htv = sem("hidden_copied_by_vector")
        s_yd = sem("down_projected")
        s_zd = sem("residual_added")
        s_vd = sem("chunk_variance_ready")
        s_rd = sem("chunk_rstd_ready")
        s_od = sem("chunk_normalised")
        s_out = [sem(f"chunk_stored{q}") for q in range(2)]
        s_dvd = sem("dve_chain_of_experts")

        block = ctx.enter_context(nc.Block())

        @block.sync
        def _(sp):
            for dst, src in ((wqkv[:, :], w_qkv), (wkvd[QR:QR + KR, :], w_kvdec), (gkv[QR:QR + KR, :], g_kv),
                             (wqd[:, :], w_qdec), (wkr[:, :], w_krope), (wqr[:, :], w_qrope),
                             (wo[:, :], w_o), (rw[:, :], router),
                             (bias_sb[:, :], bias.partition_broadcast(P)),
                             (cos_sb[:, :, :], cos.rearrange("(n p) d -> p n d", p=P)),
                             (sin_sb[:, :, :], sin.rearrange("(n p) d -> p n d", p=P))):
                sp.dma_start(dst, src).then_inc(s_w, 16)
            with sp.Fori(0, B) as b:
                sp.wait_ge(s_xtp, b)
                sp.dma_start(xn[:, :, :], x[b].rearrange("(n p) d -> p n d", p=P)).then_inc(s_x, 16)
                split = sp.snap(12 * b + 12)
                sp.wait_ge(s_hi, split)
                sp.wait_ge(s_lo, split)
                for g in range(GROUPS):
                    for stack, parts in ((ks, (hi[0], lo[0], hi[0])), (qs, (hi[1], hi[1], lo[1]))):
                        for n, part in enumerate(parts):
                            for h in range(HG * g, HG * g + HG):
                                for row, k, f, r in pieces(h):
                                    sp.dma_start(stack[n * FD + row:n * FD + row + k, h, :].bitcast(f32),
                                                 part[r:r + k, f, :].bitcast(f32)).then_inc(s_stk[g], 16)
                sp.wait_ge(s_x1, b * NT)
                sp.dma_start(xr[:, :, :], x[b].rearrange("(n p) d -> p n d", p=P)).then_inc(s_xr, 16)
                for kind, g, _ in STEPS:
                    if kind == "rows":
                        sp.wait_ge(s_mh, GROUPS * b + g + 1)
                        sp.wait_ge(s_ml, GROUPS * b + g + 1)
                        for n in range(2):
                            sp.dma_start(qs[3 * FD + n:3 * FD + n + 1, HG * g:HG * g + HG, :].bitcast(f32),
                                         rows[:, 0, n, :].bitcast(f32)).then_inc(s_row[g], 16)
                sp.wait_ge(s_x1, NT * b + NT)
                sp.dma_start(x1_dram[b].rearrange("(n p) d -> p n d", p=P), x1[:, :, :]).then_inc(s_kept, 16)
                sp.wait_ge(s_x1tc, b + 1)
                sp.dma_start(x1t_dram[b], x1t[:, :]).then_inc(s_keptt, 16)
                sp.wait_ge(s_cw, b + 1)
                sp.dma_start(cw_dram[b], cw[:, :, :].rearrange("p n e -> p (n e)")).then_inc(s_keptw, 16)
            sp.wait_ge(s_kept, 16 * B)
            sp.wait_ge(s_keptt, 16 * B)
            sp.wait_ge(s_keptw, 16 * B)
            sp.wait_ge(s_pv, GROUPS * B)
            for dst, src in ((wge, gate), (wue, up), (wsh[:, 0:HS], sgate), (wsh[:, HS:], sup),
                             (wdn[:, 0:FE].rearrange("p (k c) -> p k c", c=C), down.rearrange("(k p) c -> p k c", p=P)),
                             (wdn[:, FE:].rearrange("p (k c) -> p k c", c=C), sdown.rearrange("(k p) c -> p k c", p=P))):
                sp.dma_start(dst, src).then_inc(s_we, 16)
            with sp.Fori(0, B // 2) as i:
                for q in range(2):
                    b = 2 * i + q
                    sp.wait_ge(s_u, NT * 2 * i)
                    sp.wait_ge(s_zd, NT * 2 * i)
                    sp.dma_start(xd[q], x1_dram[b].rearrange("(n p) d -> p n d", p=P)).then_inc(s_dx[q], 16)
                    sp.dma_start(xdt[q], x1t_dram[b]).then_inc(s_dx[q], 16)
                    sp.dma_start(cwd[q].rearrange("p n e -> p (n e)"), cw_dram[b]).then_inc(s_dx[q], 16)
                for q in range(2):
                    b = 2 * i + q
                    sp.wait_ge(s_od, NT * b + NT)
                    sp.dma_start(out[b].rearrange("(n p) d -> p n d", p=P), yd[q]).then_inc(s_out[q], 16)
            for q in range(2):
                sp.wait_ge(s_out[q], 16 * (B // 2))

        @block.gpsimd
        def _(pool):
            pool.memset(ident[:, :], 0.0).then_inc(s_zero, 1)
            pool.memset(identb[:, :], 0.0).then_inc(s_zero, 1)
            pool.memset(maskb[:, :], 0.0).then_inc(s_zero, 1)
            pool.memset(lower[:, :, :], 0.0).then_inc(s_zero, 1)
            pool.memset(ones[:, :], 1.0).then_inc(s_const, 1)
            pool.memset(mhalf[:, :], -0.5).then_inc(s_const, 1)
            pool.wait_ge(s_zero, 4)
            for m in (ident, identb):
                pool.affine_select(out=m[:, :], in_=m[:, :], compare_op=ALU.not_equal, fill=1.0, base=0,
                                   pattern=[[-1, P]], channel_multiplier=1).then_inc(s_const, 1)
            pool.affine_select(out=maskb[:, :], in_=maskb[:, :], compare_op=ALU.is_ge, fill=HIDDEN, base=0,
                               pattern=[[-1, P]], channel_multiplier=1).then_inc(s_const, 1)
            pool.affine_select(out=lower[:, :, :], in_=lower[:, :, :], compare_op=ALU.is_ge, fill=1.0, base=0,
                               pattern=[[-1, E], [1, E]], channel_multiplier=0).then_inc(s_const, 1)
            with pool.Fori(0, B) as b:
                for t in range(NT):
                    pool.wait_ge(s_ms, NT * b + t + 1)
                    pool.tensor_tensor(out=rr[:, t:t + 1], in0=ms[:, t:t + 1], in1=mhalf[:, 0:1],
                                       op=ALU.pow).then_inc(s_rr, 1)
                    for n in range(2):
                        pool.wait_ge(s_prod, 6 * (NT * b + t) + 3 * n + 3)
                        rope = feat[n][:, t % 2, :, HD:]
                        pool.tensor_tensor(out=rope, in0=rope, in1=turned[n][:, t % 2, :, :],
                                           op=ALU.add).then_inc(s_rope, 1)
                for kind, u, k in STEPS:
                    if kind == "exp" and k == PS - 1:
                        pool.wait_ge(s_msk, 3 * (PAIRS * b + u))
                        pool.wait_ge(s_exp, PS * (PAIRS * b + u) + PS)
                        pool.tensor_tensor(out=tick[:, 1:2], in0=mhalf[:, 0:1], in1=mhalf[:, 0:1], op=ALU.add)
                        at = probs[:, (u // 2) % 2, :, :]
                        s = PS * (u % 2)
                        for part in (at[:, s:s + 4, 0:P], at[:, s + 1:s + 4:2, 3 * P:4 * P],
                                     at[:, s + 4, :].rearrange("p (a c) -> p a c", a=2)[:, :, 0:P]):
                            pool.affine_select(out=part, in_=part, compare_op=ALU.is_ge, fill=0.0, base=0,
                                               pattern=[[0, part.shape[1]], [1, P]],
                                               channel_multiplier=-1).then_inc(s_msk, 1)
                pool.wait_ge(s_var, b + 1)
                pool.tensor_tensor(out=rstd[:, :], in0=ve[:, :], in1=mhalf[:, :], op=ALU.pow).then_inc(s_rstd, 1)
            with pool.Fori(0, B // 2) as i:
                for q in range(2):
                    pool.wait_ge(s_dx[q], 48 * i + 48)
                    for t in range(NT):
                        n = NT * (2 * i + q) + t
                        pool.wait_ge(s_hid, 2 * n + 2)
                        h = hid[t % 2][:, 0:FE].rearrange("p (e k) -> p e k", e=E)
                        pool.tensor_tensor(out=h, in0=h, in1=cwd[q][:, t, :].unsqueeze(2).to_broadcast([P, E, HE]),
                                           op=ALU.mult).then_inc(s_hw, 1)
                    pool.wait_ge(s_vd, 2 * i + q + 1)
                    pool.tensor_tensor(out=rstd[:, :], in0=ve[:, :], in1=mhalf[:, :], op=ALU.pow).then_inc(s_rd, 1)

        @block.scalar
        def _(act):
            act.wait_ge(s_const, CONSTS)
            with act.Fori(0, B) as b:
                act.wait_ge(s_xtp, b + 1)
                act.activation(xt[:, :], psum[:, 6, :], ACT.Copy).then_inc(s_xtc, 1)
                act.wait_ge(s_qkv, b + 1)
                act.activation(qct[:, :], psum[0:QR + KR, 7, :], ACT.Copy).then_inc(s_qct, 1)
                act.activation(sq[:, :], psum[0:QR + KR, 7, :], ACT.Square).then_inc(s_qct, 1)
                act.wait_ge(s_pv, GROUPS * b)

                def contents(t):
                    p = t % 2
                    act.wait_ge(s_proj, NT * b + t + 1)
                    act.wait_ge(s_ftr, NT * b + t - 1 if t >= 2 else NT * b)
                    act.wait_ge(s_rr, NT * b + t + 1)
                    act.activation(feat[1][:, p, :, 0:HD], psum[:, 4 + p, 0:P].rearrange("p (h d) -> p h d", h=NH),
                                   ACT.Copy).then_inc(s_cont, 1)
                    act.activation(feat[0][:, p, :, 0:HD], psum[:, 4 + p, P:2 * P].rearrange("p (h d) -> p h d", h=NH), ACT.Copy,
                                   scale=rr[:, t:t + 1]).then_inc(s_cont, 1)
                    act.activation(va[:, t, :, 0:HD],
                                   psum[:, 4 + p, 2 * P:3 * P].rearrange("p (h d) -> p h d", h=NH), ACT.Copy,
                                   scale=rr[:, t:t + 1]).then_inc(s_cont, 1)

                def highs(t):
                    p = t % 2
                    act.wait_ge(s_ftr, NT * b + t + 1)
                    if t == 0:
                        for g in range(GROUPS):
                            act.wait_ge(s_stk[g], 16 * STACK_DMAS[g] * b)
                    for n in range(2):
                        act.activation(hi[n][:, 0:FB - 1, t * P:t * P + P],
                                       psum[:, 2 * p + n, :].rearrange("p (f t) -> p f t", f=NT),
                                       ACT.Copy).then_inc(s_hi, 1)
                    for n in range(2):
                        a = act.activation(hi[n][:, FB - 1, t * P:t * P + P], psum[:, 4 + p, n * P:n * P + P], ACT.Copy)
                        if n:
                            a.then_inc(s_hi, 1)

                contents(0)
                for t in range(NT):
                    if t + 1 < NT:
                        contents(t + 1)
                    highs(t)
                for kind, u, k in STEPS:
                    if kind == "exp":
                        n = PS * u + k
                        act.wait_ge(s_st, PS * PAIRS * b + n + 1)
                        if n % (2 * PS) == 0:
                            act.wait_ge(s_pv, GROUPS * b + u // 2 - 1 if u >= 4 else GROUPS * b)
                        act.activation(probs[:, (u // 2) % 2, PS * (u % 2) + k, :], psum[:, 4 + n % 2, :], ACT.Exp,
                                       scale=SCALE).then_inc(s_exp, 1)
                    elif kind == "rows":
                        act.wait_ge(s_nmt, GROUPS * b + u + 1)
                        act.wait_ge(s_row[(u - 1) % GROUPS], 32 * b + 32 if u else 32 * b)
                        act.activation(rows[:, 0, 0, :], psum[0:HG, 7, :], ACT.Copy).then_inc(s_mh, 1)
                    elif kind == "pv":
                        act.wait_ge(s_pv, GROUPS * b + u + 1)
                        act.wait_ge(s_otr, GROUPS * b + u - 1 if u >= 2 else GROUPS * b)
                        act.activation(ot[:, u % 2, :], psum[:, 6, :], ACT.Copy).then_inc(s_oc, 1)
                act.wait_ge(s_ont, b + 1)
                act.activation(ont[:, :], psum[:, 7, :], ACT.Copy).then_inc(s_ontc, 1)
                act.wait_ge(s_x1tp, b + 1)
                act.wait_ge(s_keptt, 16 * b)
                act.activation(x1t[:, :], psum[:, 7, :], ACT.Copy).then_inc(s_x1tc, 1)
                act.wait_ge(s_lg, b + 1)
                act.wait_ge(s_cw, b)
                act.activation(sc[:, :, :], psum[:, 6, 0:NT * E].rearrange("p (n e) -> p n e", n=NT), ACT.Exp,
                               scale=-1.0).then_inc(s_el, 1)

            def copy_hidden(n, t):
                act.wait_ge(s_ht, n + 1)
                act.activation(hidt[t % 2][:, 0:4, :], psum[:, 6, :].rearrange("p (k t) -> p k t", k=4),
                               ACT.Copy).then_inc(s_hta, 1)

            with act.Fori(0, B // 2) as i:
                for m in range(2 * NT):
                    n = 2 * NT * i + m
                    p = m % 2
                    act.wait_ge(s_g, n + 1)
                    act.wait_ge(s_hid, 2 * (n - 1) if m >= 2 else 2 * NT * 2 * i)
                    act.activation(act_out[p][:, 0:FE], psum[:, 3 * p, :], ACT.Silu).then_inc(s_act, 1)
                    if m:
                        copy_hidden(n - 1, m - 1)
                    act.wait_ge(s_u, n + 1)
                    act.activation(act_out[p][:, FE:FH], psum[:, 3 * p + 2, 0:HS], ACT.Silu).then_inc(s_act, 1)
                copy_hidden(2 * NT * i + 2 * NT - 1, 2 * NT - 1)

        @block.vector
        def _(dve):
            dve.memset(ks[96:P, :, :].bitcast(f32), 1.0).then_inc(s_const, 1)
            dve.memset(va[:, :, :, :], 0.0).then_inc(s_zeroed, 1)
            dve.wait_ge(s_zeroed, 1)
            dve.memset(va[:, :, :, HD:HD + 1], 1.0).then_inc(s_const, 1)
            dve.wait_ge(s_w, 16 * 11)
            dve.tensor_scalar(wkvg[QR:QR + KR, :], wkvd[QR:QR + KR, :], gkv[QR:QR + KR, 0:1], None,
                              ALU.mult).then_inc(s_const, 1)
            LINKS = 54
            with dve.Fori(0, B) as b:
                linked = [0]

                def link(ins):
                    linked[0] += 1
                    ins.then_inc(s_dve, 1)
                    dve.wait_ge(s_dve, LINKS * b + linked[0])

                def products(t):
                    p = t % 2
                    dve.wait_ge(s_proj, NT * b + t + 1)
                    dve.wait_ge(s_cont, 12 * b)
                    dve.tensor_scalar(ms[:, t:t + 1], psum[:, 4 + p, 3 * P:3 * P + 1], 1.0 / KR, RMS_EPS,
                                      ALU.mult, ALU.add).then_inc(s_ms, 1)
                    dve.wait_ge(s_ftr, NT * b + t - 1 if t >= 2 else NT * b)
                    for n in range(2):
                        src = psum[:, 2 * p + n, :].rearrange("p (h d) -> p h d", h=NH)
                        H = RD // 2
                        dve.tensor_tensor(feat[n][:, p, :, HD:], src,
                                          cos_sb[:, t, :].unsqueeze(1).to_broadcast([P, NH, RD]),
                                          ALU.mult).then_inc(s_prod, 1)
                        for a, c in ((0, H), (H, 0)):
                            dve.tensor_tensor(turned[n][:, p, :, a:a + H], src[:, :, c:c + H],
                                              sin_sb[:, t, a:a + H].unsqueeze(1).to_broadcast([P, NH, H]),
                                              ALU.mult).then_inc(s_prod, 1)

                def lows(t):
                    p = t % 2
                    for n in range(3):
                        dve.wait_ge(s_hi, 12 * b + 3 * t + n + 1)
                        if n < 2:
                            at = hi[n][:, 0:FB - 1, t * P:t * P + P], lo[n][:, 0:FB - 1, t * P:t * P + P]
                            dve.tensor_tensor(at[1], psum[:, 2 * p + n, :].rearrange("p (f t) -> p f t", f=NT),
                                              at[0].bitcast(f32), ALU.subtract).then_inc(s_lo, 1)
                        else:
                            for m in range(2):
                                a = dve.tensor_tensor(lo[m][:, FB - 1, t * P:t * P + P],
                                                      psum[:, 4 + p, m * P:m * P + P],
                                                      hi[m][:, FB - 1, t * P:t * P + P].bitcast(f32), ALU.subtract)
                            a.then_inc(s_lo, 1)

                products(0)
                for t in range(NT):
                    if t + 1 < NT:
                        products(t + 1)
                    lows(t)
                for kind, u, k in STEPS:
                    if kind == "max":
                        n = 3 * u + k
                        g, h = u // 2, 2 * (u % 2)
                        dve.wait_ge(s_mx, 3 * PAIRS * b + n + 1)
                        if k == 0 and u % 2 == 0:
                            dve.wait_ge(s_nmt, GROUPS * b + g - 1 if g >= 2 else GROUPS * b)
                        slot = psum[:, 2 * (n % 2):2 * (n % 2) + 2, :]
                        for qt, c in MAX_STEPS[k]:
                            w = (qt + 1) * P
                            src = (psum[:, 2 * (n % 2), :].rearrange("p (a c) -> p a c", a=2) if qt == 1
                                   else slot[:, :, c:c + w])
                            a = dve.tensor_reduce(nm[:, g % 2, qt, h:h + 2], src, AX.X, ALU.max, negate=True)
                        a.then_inc(s_mxr, 1)
                    elif kind == "rows":
                        dve.wait_ge(s_mh, GROUPS * b + u + 1)
                        dve.tensor_tensor(rows[:, 0, 1, :], psum[0:HG, 7, :], rows[:, 0, 0, :].bitcast(f32),
                                          ALU.subtract).then_inc(s_ml, 1)
                    elif kind == "turn":
                        dve.wait_ge(s_otr, GROUPS * b + u + 1)
                        heads = psum[:, 7, :].rearrange("p (n h c) -> p n h c", n=NT, h=HG)
                        link(dve.reciprocal(rs[:, :, :].unsqueeze(3), heads[:, :, :, HD:HD + 1]))
                        dve.tensor_tensor(on[:, :, HG * u:HG * u + HG, :], heads[:, :, :, 0:HD],
                                          rs[:, :, :].unsqueeze(3).to_broadcast([P, NT, HG, HD]),
                                          ALU.mult).then_inc(s_on, 1)
                dve.wait_ge(s_y, b + 1)
                dve.wait_ge(s_xr, 16 * b + 16)
                link(dve.tensor_tensor(z[:, :, :], psum[:, 6, :].rearrange("p (n d) -> p n d", n=NT), xr[:, :, :], ALU.add))
                for t in range(NT):
                    a = dve.bn_stats(st6[:, t, :], z[:, t, :])
                link(a)
                dve.tensor_copy(tick[:, 0:1], mhalf[:, 0:1])
                for t in range(NT):
                    a = dve.bn_aggr(mv[:, t, :], st6[:, t, :])
                link(a)
                dve.tensor_scalar(ve[:, :].unsqueeze(2), mv[:, :, 1:2], LN_EPS, None, ALU.add).then_inc(s_var, 1)
                dve.wait_ge(s_rstd, b + 1)
                dve.wait_ge(s_kept, 16 * b)
                for t in range(NT):
                    dve.tensor_scalar(x1[:, t, :], z[:, t, :], mv[:, t, 0:1], rstd[:, t:t + 1], ALU.subtract,
                                      ALU.mult).then_inc(s_x1, 1)
                dve.wait_ge(s_el, b + 1)
                link(dve.tensor_scalar(sc[:, :, :], sc[:, :, :], 1.0, None, ALU.add))
                link(dve.reciprocal(sc[:, :, :], sc[:, :, :]))
                link(dve.tensor_tensor(sbias[:, :, :], sc[:, :, :],
                                       bias_sb[:, :].unsqueeze(1).to_broadcast([P, NT, E]), ALU.add))
                four = sbias[:, :, :].rearrange("p n (g e) -> p (n g) e", g=NG)
                a0, a1, a2, a3 = (four[:, :, i:i + 1] for i in range(EG))
                s0, s1, s2, s3, s4, s5 = (t2[:, i, :].unsqueeze(2) for i in range(6))
                dve.tensor_tensor(s0, a0, a1, ALU.max)
                dve.tensor_tensor(s1, a0, a1, ALU.min)
                dve.tensor_tensor(s2, a2, a3, ALU.max)
                link(dve.tensor_tensor(s3, a2, a3, ALU.min))
                dve.tensor_tensor(s4, s0, s2, ALU.min)
                link(dve.tensor_tensor(s5, s1, s3, ALU.max))
                link(dve.tensor_tensor(s1, s0, s2, ALU.max))
                link(dve.tensor_tensor(s3, s4, s5, ALU.max))
                link(dve.tensor_tensor(s0, s1, s3, ALU.add))
                gs = t2[:, 0, :].rearrange("p (n g) -> p n g", n=NT)
                NG2 = NG * NG

                def ranked(vals, n, out_, tiles):
                    for i in tiles:
                        mine = vals[:, i, :].unsqueeze(2).to_broadcast([P, n, n])
                        other = vals[:, i, :].unsqueeze(1).to_broadcast([P, n, n])
                        eq, gt = big[:, 0, 0:n, 0:n], big[:, 1, 0:n, 0:n]
                        dve.tensor_tensor(gt, other, mine, ALU.is_gt)
                        link(dve.tensor_tensor(eq, other, mine, ALU.is_equal))
                        link(dve.tensor_tensor(eq, eq, lower[:, 0:n, 0:n], ALU.mult))
                        link(dve.tensor_tensor(gt, gt, eq, ALU.add))
                        link(dve.tensor_reduce(out_[:, i, :], gt, AX.X, ALU.add))

                ranked(gs, NG, gmask, range(NT))
                link(dve.tensor_scalar(gmask[:, :, :], gmask[:, :, :], TOPG - 0.5, -3e38, ALU.is_gt, ALU.mult))
                link(dve.tensor_tensor(masked[:, :, :].rearrange("p n (g e) -> p (n g) e", g=NG), four,
                                       gmask[:, :, :].rearrange("p n g -> p (n g)").unsqueeze(2).to_broadcast([P, NT * NG, EG]),
                                       ALU.add))
                ranked(masked, E, rank, range(NT))
                link(dve.tensor_scalar(rank[:, :, :], rank[:, :, :], TOPK - 0.5, None, ALU.is_lt))
                link(dve.tensor_tensor(rank[:, :, :], rank[:, :, :], sc[:, :, :], ALU.mult))
                link(dve.tensor_reduce(wsum[:, 0, :], rank[:, :, :], AX.X, ALU.add))
                link(dve.tensor_scalar(wsum[:, 0, :], wsum[:, 0, :], 1e-20, None, ALU.add))
                link(dve.reciprocal(wsum[:, 1, :], wsum[:, 0, :]))
                dve.wait_ge(s_keptw, 16 * b)
                dve.tensor_tensor(cw[:, :, :], rank[:, :, :], wsum[:, 1, :].unsqueeze(2).to_broadcast([P, NT, E]),
                                  ALU.mult).then_inc(s_cw, 1)
                assert linked[0] == LINKS

            DLINKS = 4
            with dve.Fori(0, B // 2) as i:
                linkd = [0]

                def linkx(ins):
                    linkd[0] += 1
                    ins.then_inc(s_dvd, 1)
                    dve.wait_ge(s_dvd, DLINKS * i + linkd[0])

                def down_out(m):
                    n, q, t = 2 * NT * i + m, m // NT, m % NT
                    dve.wait_ge(s_ht, n + 1)
                    dve.tensor_copy(hidt[m % 2][:, 4:HB, :],
                                    psum[:, 7, 0:HS].rearrange("p (k t) -> p k t", k=HB - 4)).then_inc(s_htv, 1)
                    dve.wait_ge(s_yd, n + 1)
                    dve.tensor_tensor(zd[q][:, t, :], psum[:, 7, HS:HS + C], xd[q][:, t, :], ALU.add).then_inc(s_zd, 1)

                def norm(q):
                    b = 2 * i + q
                    dve.wait_ge(s_zd, NT * b + NT)
                    for t in range(NT):
                        a = dve.bn_stats(st6[:, t, :], zd[q][:, t, :])
                    linkx(a)
                    dve.tensor_copy(tick[:, 0:1], mhalf[:, 0:1])
                    for t in range(NT):
                        a = dve.bn_aggr(mv[:, t, :], st6[:, t, :])
                    linkx(a)
                    dve.tensor_scalar(ve[:, :].unsqueeze(2), mv[:, :, 1:2], LN_EPS, None, ALU.add).then_inc(s_vd, 1)
                    dve.wait_ge(s_rd, b + 1)
                    dve.wait_ge(s_out[q], 16 * i)
                    for t in range(NT):
                        dve.tensor_scalar(yd[q][:, t, :], zd[q][:, t, :], mv[:, t, 0:1], rstd[:, t:t + 1],
                                          ALU.subtract, ALU.mult).then_inc(s_od, 1)

                for m in range(2 * NT):
                    n, p = 2 * NT * i + m, m % 2
                    if m % NT == 0:
                        dve.wait_ge(s_dx[m // NT], 48 * i + 48)
                    if m:
                        down_out(m - 1)
                    dve.wait_ge(s_ht, n - 1 if m >= 2 else 2 * NT * i)
                    for c in range(2):
                        dve.wait_ge(s_act, 2 * n + c + 1)
                        dve.wait_ge(s_u, n + 1)
                        a, b_, src = ((0, FE, psum[:, 3 * p + 1, :]), (FE, FH, psum[:, 3 * p + 2, HS:]))[c]
                        dve.tensor_tensor(hid[p][:, a:b_], src, act_out[p][:, a:b_], ALU.mult).then_inc(s_hid, 1)
                    if m == NT:
                        norm(0)
                down_out(2 * NT - 1)
                norm(1)
                assert linkd[0] == DLINKS

        @block.tensor
        def _(pe):
            pe.wait_ge(s_w, 16 * 11)
            pe.wait_ge(s_const, CONSTS)
            with pe.Fori(0, B) as b:
                pe.wait_ge(s_x, 16 * b + 16)
                pe.wait_ge(s_el, b)
                for t in range(NT):
                    a = pe.transpose(psum[:, 6, t * P:t * P + P], xn[:, t, :], ident[:, :])
                a.then_inc(s_xtp, 1)
                pe.wait_ge(s_xtc, b + 1)
                pe.wait_ge(s_x1tc, b)
                pe.matmul(psum[0:QR + KR, 7, :], wqkv[:, :], xt[:, :], start=True, stop=True).then_inc(s_qkv, 1)

                def project(t):
                    p = t % 2
                    at = slice(t * P, t * P + P)
                    if t >= 2:
                        pe.wait_ge(s_hi, 12 * b + 3 * (t - 2) + 3)
                        pe.wait_ge(s_lo, 12 * b + 3 * (t - 2) + 3)
                    else:
                        pe.wait_ge(s_mxr, 3 * PAIRS * b)
                        pe.wait_ge(s_exp, PS * PAIRS * b)
                    pe.matmul(psum[:, 2 * p, :], xt[:, at], wkr[:, :], start=True, stop=True)
                    if t == 0:
                        pe.wait_ge(s_qct, 2 * b + 2)
                    pe.matmul(psum[:, 2 * p + 1, :], qct[0:QR, at], wqr[:, :], start=True, stop=True)
                    pe.matmul(psum[:, 4 + p, 0:P], qct[0:QR, at], wqd[:, :], start=True, stop=True)
                    pe.matmul(psum[:, 4 + p, P:3 * P], qct[QR:QR + KR, at], wkvg[QR:QR + KR, :], start=True, stop=True)
                    pe.matmul(psum[:, 4 + p, 3 * P:3 * P + 1], sq[QR:QR + KR, at], ones[QR:QR + KR, :],
                              start=True, stop=True).then_inc(s_proj, 1)

                def turn_features(t):
                    p = t % 2
                    pe.wait_ge(s_rope, 2 * (NT * b + t) + 2)
                    pe.wait_ge(s_cont, 12 * b + 3 * t + 3)
                    both = [v[:, p, :, :].rearrange("p h d -> p (h d)") for v in feat]
                    for n in range(2):
                        for f in range(FB - 1):
                            pe.transpose(psum[:, 2 * p + n, f * P:f * P + P], both[n][:, f * P:f * P + P], ident[:, :])
                    for n in range(2):
                        a = pe.transpose(psum[:, 4 + p, n * P:n * P + P], both[n][:, (FB - 1) * P:], ident[:, :])
                    a.then_inc(s_ftr, 1)

                project(0)
                for t in range(NT):
                    if t + 1 < NT:
                        project(t + 1)
                    turn_features(t)

                for kind, u, k in STEPS:
                    if kind == "max":
                        n = 3 * u + k
                        if n < 2:
                            pe.wait_ge(s_hi, 12 * b + 12)
                            pe.wait_ge(s_lo, 12 * b + 12)
                        else:
                            pe.wait_ge(s_mxr, 3 * PAIRS * b + n - 1)
                        if k == 0 and u % 2 == 0:
                            pe.wait_ge(s_stk[u // 2], 16 * STACK_DMAS[u // 2] * (b + 1))
                        for qt, c in MAX_STEPS[k]:
                            w = (qt + 1) * P
                            for i in range(2):
                                dst = (psum[:, 2 * (n % 2), i * w:i * w + w] if qt == 1
                                       else psum[:, 2 * (n % 2) + i, c:c + w])
                                pe.matmul(dst, qs[0:3 * FD, 2 * u + i, qt * P:qt * P + P],
                                          ks[0:3 * FD, 2 * u + i, 0:w], start=True, stop=False)
                                a = pe.matmul(dst[:, w - P:w], identb[:, :], maskb[:, :], start=False, stop=True)
                        a.then_inc(s_mx, 1)
                    elif kind == "rows":
                        pe.wait_ge(s_mxr, 3 * (PAIRS * b + 2 * u + 2))
                        if u:
                            pe.wait_ge(s_ml, GROUPS * b + u)
                            pe.wait_ge(s_on, GROUPS * b + u - 1)
                        for qt in range(NT):
                            a = pe.matmul(psum[0:HG, 7, qt * P:qt * P + P], nm[:, u % 2, qt, :], ident[:, :],
                                          start=True, stop=True)
                        a.then_inc(s_nmt, 1)
                    elif kind == "exp":
                        n = PS * u + k
                        if n >= 2:
                            pe.wait_ge(s_exp, PS * PAIRS * b + n - 1)
                        if k == 0 and u % 2 == 0:
                            pe.wait_ge(s_row[u // 2], 32 * b + 32)
                        for i, kt, c in EXP_STEPS[k]:
                            h = 2 * u + i
                            w = T - kt * P
                            a = pe.matmul(psum[:, 4 + n % 2, c:c + w], ks[0:3 * FD + 2, h, kt * P:kt * P + P],
                                          qs[0:3 * FD + 2, h, kt * P:T], start=True, stop=True)
                        a.then_inc(s_st, 1)
                    elif kind == "pv":
                        pe.wait_ge(s_msk, 6 * (GROUPS * b + u) + 6)
                        pe.wait_ge(s_oc, GROUPS * b + u)
                        for kt in range(NT):
                            for j in range(HG):
                                i, s = j % 2, PS * (j // 2)
                                slot, c = ((s + 4, 2 * P * i) if kt == 2 else
                                           (s + 2 * i + (kt > 0), 3 * P if kt == 3 else 0))
                                w = T - kt * P
                                a = pe.matmul(psum[SLOT * j:SLOT * j + SLOT, 6, kt * P:T], va[:, kt, HG * u + j, :],
                                              probs[:, u % 2, slot, c:c + w], start=kt == 0, stop=kt == NT - 1)
                        a.then_inc(s_pv, 1)
                    else:
                        pe.wait_ge(s_oc, GROUPS * b + u + 1)
                        pe.wait_ge(s_ml, GROUPS * b + min(u + 2, GROUPS))
                        pe.wait_ge(s_on, GROUPS * b + u)
                        for qt in range(NT):
                            a = pe.transpose(psum[:, 7, qt * P:qt * P + P], ot[:, u % 2, qt * P:qt * P + P], ident[:, :])
                        a.then_inc(s_otr, 1)

                pe.wait_ge(s_on, GROUPS * b + GROUPS)
                for t in range(NT):
                    a = pe.transpose(psum[:, 7, t * P:t * P + P], on[:, t, :, :].rearrange("p h d -> p (h d)"), ident[:, :])
                a.then_inc(s_ont, 1)
                pe.wait_ge(s_ontc, b + 1)
                for t in range(NT):
                    a = pe.matmul(psum[:, 6, t * P:t * P + P], ont[:, t * P:t * P + P], wo[:, :], start=True, stop=True)
                a.then_inc(s_y, 1)
                pe.wait_ge(s_x1, NT * b + NT)
                for t in range(NT):
                    a = pe.transpose(psum[:, 7, t * P:t * P + P], x1[:, t, :], ident[:, :])
                a.then_inc(s_x1tp, 1)
                pe.wait_ge(s_x1tc, b + 1)
                for t in range(NT):
                    a = pe.matmul(psum[:, 6, t * E:t * E + E], x1t[:, t * P:t * P + P], rw[:, :], start=True, stop=True)
                a.then_inc(s_lg, 1)

            pe.wait_ge(s_we, 16 * 6)
            pe.wait_ge(s_el, B)
            pe.wait_ge(s_mxr, 3 * PAIRS * B)

            def gates(i, m):
                q, t, p = m // NT, m % NT, m % 2
                if t == 0:
                    pe.wait_ge(s_dx[q], 48 * i + 48)
                pe.wait_ge(s_hid, 2 * (2 * NT * i + m - 1) if m >= 2 else 2 * 2 * NT * i)
                pe.matmul(psum[:, 3 * p, :], xdt[q][:, t * P:t * P + P], wge, start=True, stop=True).then_inc(s_g, 1)

            def ups(m):
                q, t, p = m // NT, m % NT, m % 2
                pe.matmul(psum[:, 3 * p + 1, :], xdt[q][:, t * P:t * P + P], wue, start=True, stop=True)
                pe.matmul(psum[:, 3 * p + 2, :], xdt[q][:, t * P:t * P + P], wsh, start=True, stop=True).then_inc(s_u, 1)

            with pe.Fori(0, B // 2) as i:
                gates(i, 0)
                ups(0)
                for m in range(2 * NT):
                    n, p = 2 * NT * i + m, m % 2
                    pe.wait_ge(s_hw, n + 1)
                    pe.wait_ge(s_hta, n)
                    pe.wait_ge(s_zd, n)
                    for k in range(HB):
                        a = pe.transpose(psum[:, 6 + k // 4, (k % 4) * P:(k % 4) * P + P],
                                         hid[p][:, k * P:k * P + P], ident[:, :])
                    a.then_inc(s_ht, 1)
                    if m + 1 < 2 * NT:
                        gates(i, m + 1)
                    pe.wait_ge(s_hta, n + 1)
                    pe.wait_ge(s_htv, n + 1)
                    for k in range(HB):
                        a = pe.matmul(psum[:, 7, HS:HS + C], hidt[p][:, k, :], wdn[:, k * C:k * C + C],
                                      start=k == 0, stop=k == HB - 1)
                    a.then_inc(s_yd, 1)
                    if m + 1 < 2 * NT:
                        ups(m + 1)


def kernel(**inputs):
    import numpy as _np
    import concourse.bacc as _bacc
    from concourse import mybir as _mybir
    from concourse.bass_utils import run_bass_kernel_spmd as _run

    f = {k.split("_", 2)[2]: _np.asarray(v) for k, v in inputs.items() if k.startswith("L0_ffn")}
    a = {k.split("_", 2)[2]: _np.asarray(v) for k, v in inputs.items() if k.startswith("L0_attn")}

    inv_freq = 1.0 / 10000.0 ** (_np.arange(0, RD, 2, dtype=_np.float32) / RD)
    freqs = _np.outer(_np.arange(T, dtype=_np.float32), inv_freq)
    emb = _np.concatenate([freqs, freqs], -1)
    sign = _np.where(_np.arange(RD) < RD // 2, -1.0, 1.0)
    arrays = {
        "x": a["x"],
        "w_qkv": _np.concatenate([a["W_q"], a["W_kv"]], 1),
        "w_kvdec": _np.concatenate([a["W_kdec"], a["W_vdec"]], 1),
        "g_kv": a["g_kv"].reshape(KR, 1),
        "w_qdec": a["W_qdec"],
        "w_krope": a["W_krope"],
        "w_qrope": a["W_qrope"],
        "w_o": a["W_o"],
        "router": f["router_w"].T,
        "bias": f["correction_bias"],
        "gate": f["gate_w"].transpose(1, 0, 2).reshape(C, E * HE),
        "up": f["up_w"].transpose(1, 0, 2).reshape(C, E * HE),
        "down": f["down_w"].reshape(E * HE, C),
        "sgate": f["shared_gate_w"].T,
        "sup": f["shared_up_w"].T,
        "sdown": f["shared_down_w"].T,
        "cos": _np.cos(emb).astype(_np.float32),
        "sin": (_np.sin(emb) * sign).astype(_np.float32),
    }
    nc = _bacc.Bacc("TRN2", target_bir_lowering=False, num_devices=1)
    f32 = _mybir.dt.float32
    sent, args = {}, []
    for name, v in arrays.items():
        sent["in_" + name] = _np.ascontiguousarray(v)
        args.append(nc.dram_tensor("in_" + name, v.shape, f32, kind="ExternalInput").ap())
    args.append(nc.dram_tensor("out_0", (B, T, C), f32, kind="ExternalOutput").ap())
    args.append(nc.dram_tensor("x1_kept", (B, T, C), f32, kind="Internal").ap())
    args.append(nc.dram_tensor("x1t_kept", (B, C, T), f32, kind="Internal").ap())
    args.append(nc.dram_tensor("weights_kept", (B, P, NT * E), f32, kind="Internal").ap())
    mla_moe_kernel(nc, *args)
    r = _run(nc, [sent], core_ids=[0])
    return r.results[0]["out_0"]
```

```python
import concourse.bass as bass
from concourse import mybir
from contextlib import ExitStack

B, T, C = 16, 512, 128
NH, HD, RD = 16, 8, 32
FD = HD + RD
QR, KR = 64, 32
E, NG, HE = 16, 4, 32
EG = E // NG
TOPG, TOPK = 2, 4
HS = 256
P = 128
NT = T // P
RMS_EPS, LN_EPS = 1e-6, 1e-5
BH = P // FD
FR = BH * FD
SLOTS = (2 * NH + BH - 1) // BH * BH
FB = SLOTS // BH
HG = 4
GROUPS = NH // HG
PAIRS = NH // 2
SCALE = 1.0 / float(FD) ** 0.5
HIDDEN = -1e30
SLOT = 32
VW = HD + 1
PS = 5

MAX_STEPS = (((0, 3, 0),), ((0, 2, 0), (0, 0, 384)), ((1, 3, 0),), ((1, 2, 0), (1, 0, 384)),
             ((0, 1, 0), (1, 1, 256)))
EXP_STEPS = (((0, 0, 0),), ((0, 1, 0), (0, 3, 384)), ((1, 0, 0),), ((1, 1, 0), (1, 3, 384)),
             ((0, 2, 0), (1, 2, 256)))
SB = PS * PAIRS
HALVES = 2
CHUNKS = 6
AHEAD = 13


def steady_steps():
    at = [[] for _ in range(SB)]

    def put(step, *item):
        at[step].append(item)

    put(0, "load_x", 1, 0, 0)
    put(0, "load_residual", -1, 0, 0)
    for n in range(CHUNKS):
        put(n // 2, "stack", 0, 1, n)
        put(22 + n, "stack", 1, 0, n)
    put(1, "turn_x", 1, 0, 0)
    put(2, "latents", 1, 0, 0)
    put(5, "values", 0, 0, 0)
    for t, (k, q, c, f) in enumerate(((3, 4, 5, (7, 8, 9)), (6, 8, 9, (12, 13, 14)),
                                      (10, 11, 14, (16, 17, 18)), (15, 16, 17, (19, 20, 21)))):
        put(k, "k_rope", 1, t, 0)
        put(q, "q_rope", 1, t, 0)
        put(c, "contents", 1, t, 0)
        for n in range(3):
            put(f[n], "features", 1, t, n)
    for g in range(GROUPS):
        put((10 * g + 13) % SB, "pv", 0 if 10 * g + 13 < SB else -1, g, 0)
        put((10 * g + 15) % SB, "turn", 0 if 10 * g + 15 < SB else -1, g, 0)
        put((10 * g - 3) % SB, "rows", 0 if g else 1, g, 0)
    put(6, "turn_heads", -1, 0, 0)
    put(7, "project_out", -1, 0, 0)
    put(9, "x1", -1, 0, 0)
    put(11, "turn_x1", -1, 0, 0)
    put(12, "logits", -1, 0, 0)
    for n in range(7):
        put(21 + 2 * n, "route", -1, n, 0)
    steps = []
    for n in range(SB):
        m = n + AHEAD
        steps.append(("max", m // SB, m % SB // PS, m % PS))
        steps += at[n]
        steps.append(("exp", 0, n // PS, n % PS))
    return steps


STEADY = steady_steps()
ITEMS = {phase: [item for item in STEADY if item[1] in batches] for phase, batches in
         (("before", (1,)), ("first", (0, 1)), ("steady", (-1, 0, 1)), ("last", (-1, 0)), ("after", (-1,)))}
SCRATCH = ("turn_x", "latents", "k_rope", "q_rope", "contents", "features", "turn_heads",
           "project_out", "turn_x1", "logits")
SCRATCH_BANKS = (2, 3)


def scratch_uses(b, phase):
    def uses(p):
        return [item for item in ITEMS[p] if item[0] in SCRATCH]

    n0, n1, n2, n3 = (len(uses(p)) // 2 for p in ("before", "first", "steady", "last"))
    start = {"before": 0, "first": n0, "steady": n2 * (b - 1) + (n0 + n1), "last": n0 + n1 + n2 * (B - 2),
             "after": n0 + n1 + n2 * (B - 2) + n3}[phase]
    return {item: (n % 2, start + (n // 2 + 1)) for n, item in enumerate(uses(phase))}


def slots_of(n, i, half):
    heads = [h for h in range(NH * half // HALVES, NH * (half + 1) // HALVES) if (n * NH + h) % BH == i]
    return heads[0], heads[-1] + 1, (n * NH + heads[0]) // BH, (n * NH + heads[-1]) // BH + 1


STACKED = 16 * CHUNKS * BH


def after(engine, semaphore, value):
    if not isinstance(value, int) or value > 0:
        engine.wait_ge(semaphore, value)


def mla_moe_kernel(nc, x, w_qkv, w_kvdec, g_kv, w_qdec, w_krope, w_qrope, w_o, router, bias,
                   gate, up, down, sgate, sup, sdown, cos, sin, out, x1_dram, x1t_dram, cw_dram):
    f32, f32r, bf16 = mybir.dt.float32, mybir.dt.float32r, mybir.dt.bfloat16
    ALU, ACT, AX = mybir.AluOpType, mybir.ActivationFunctionType, mybir.AxisListType
    ctx = ExitStack()

    def sb(name, shape, dt=f32):
        return ctx.enter_context(nc.sbuf_tensor(name, shape, dt))

    def sem(name):
        return ctx.enter_context(nc.semaphore(name))

    with ctx:
        wqkv = sb("wqkv", [P, QR + KR])
        wkvg = sb("wkvg", [QR + KR, 2 * P])
        gkv = sb("gkv", [QR + KR, 1])
        ones = sb("ones", [QR + KR, 1])
        wqd = sb("wqd", [QR, P])
        wkr = sb("wkr", [P, RD * NH])
        wqr = sb("wqr", [QR, RD * NH])
        wo = sb("wo", [P, C])
        rw = sb("rw", [P, E])
        bias_sb = sb("bias_sb", [P, E])
        cos_sb = sb("cos_sb", [P, NT, RD])
        sin_sb = sb("sin_sb", [P, NT, RD])
        ident = sb("ident", [P, P])
        identb = sb("identb", [P, P], bf16)
        maskb = sb("maskb", [P, P], bf16)
        lower = sb("lower", [P, E, E])
        mhalf = sb("mhalf", [P, NT])
        tick = sb("tick", [P, 2])
        xn = sb("xn", [P, NT, C])
        xr = sb("xr", [P, NT, C])
        xt = sb("xt", [P, T])
        qct = sb("qct", [QR + KR, T])
        sq = sb("sq", [QR + KR, T])
        ms = sb("ms", [P, NT])
        rr = sb("rr", [P, NT])
        feat = sb("feat", [P, 2, SLOTS, FD])
        turned = [sb("tk", [P, NH, RD]), sb("tq", [P, NH, RD])]
        hi = sb("hi", [P, FB, T], f32r)
        lo = sb("lo", [P, FB, T], f32r)
        ks = sb("ks", [P, NH, T], f32r)
        qs = sb("qs", [P, NH, T], f32r)
        vn = sb("vn", [P, NT, NH, HD])
        va = sb("va", [P, NT, NH * VW + SLOT - VW])
        probs = sb("probs", [P, 2, 2 * PS, T])
        nm = sb("nm", [P, 2, NT, HG])
        rows = sb("rows", [HG, 1, 2, T], f32r)
        ot = sb("ot", [P, T])
        rs = sb("rs", [P, NT, HG])
        on = sb("on", [P, NT, NH, HD])
        st6 = sb("st6", [P, NT, 6])
        mv = sb("mv", [P, NT, 2])
        ve = sb("ve", [P, NT])
        rstd = sb("rstd", [P, NT])
        x1 = sb("x1", [P, NT, C])
        x1t = sb("x1t", [P, T])
        ont = x1t
        z = xr
        sc = sb("sc", [P, NT, E])
        sbias = sb("sbias", [P, NT, E])
        t2 = sb("t2", [P, 8, NT * NG])
        gmask = sb("gmask", [P, NT, NG])
        masked = sb("masked", [P, NT, E])
        above = sb("above", [P, E, E])
        equal = sb("equal", [P, E, E])
        rank = sb("rank", [P, NT, E])
        cw = sb("cw", [P, NT, E])
        wsum = sb("wsum", [P, 2, NT])

        wkvd = probs[:, 0, 0, :]
        psum = ctx.enter_context(nc.psum_tensor("psum", [P, 8, T], f32))

        s_w = sem("weights_loaded")
        s_zero = sem("pool_zeroed")
        s_const = sem("constants_made")
        CONSTS = 9
        s_x = sem("x_loaded")
        s_xr = sem("residual_loaded")
        s_made = [sem(f"scratch{k}_made") for k in range(2)]
        s_read = [sem(f"scratch{k}_read") for k in range(2)]
        s_qct = sem("latents_copied")
        s_ms = sem("mean_square_ready")
        s_rr = sem("inverse_rms_ready")
        s_vn = sem("next_values_copied")
        s_va = sem("values_in_place")
        s_rope = sem("rotary_added")
        s_hi = sem("high_parts_ready")
        s_stk = [sem(f"stacked{n}") for n in range(HALVES)]
        s_mx = sem("max_scores_made")
        s_mxr = sem("maxima_taken")
        s_nmt = sem("maxima_transposed")
        s_mh = sem("max_hi_ready")
        s_ml = sem("max_lo_ready")
        s_row = [sem(f"max_rows_placed{g}") for g in range(GROUPS)]
        s_st = sem("scores_made")
        s_exp = sem("exponentials_ready")
        s_msk = sem("future_zeroed")
        s_pv = sem("values_weighted")
        s_oc = sem("weighted_copied")
        s_otr = sem("weighted_transposed")
        s_rs = sem("inverse_sums_ready")
        s_on = sem("heads_normalised")
        s_var = sem("variance_ready")
        s_rstd = sem("rstd_ready")
        s_x1 = sem("x1_ready")
        s_cw = sem("expert_weights_ready")
        s_kept = sem("x1_stored")
        s_keptt = sem("x1t_stored")
        s_keptw = sem("expert_weights_stored")
        s_dve = sem("dve_chain")

        FE = E * HE
        FH = FE + HS
        HB = FH // P
        arena = probs[:, :, :, :].rearrange("p a s t -> p (a s t)")
        taken = [0]

        def view(size):
            taken[0] += size
            return arena[:, taken[0] - size:taken[0]]

        wge, wue, wsh, wdn = view(FE), view(FE), view(2 * HS), view(FH)
        xd = [view(NT * C).rearrange("p (n d) -> p n d", n=NT) for _ in range(2)]
        xdt = [view(T) for _ in range(2)]
        cwd = [view(NT * E).rearrange("p (n e) -> p n e", n=NT) for _ in range(2)]
        act_out = [view(FH) for _ in range(2)]
        hid = [view(FH) for _ in range(2)]
        hidt = [view(FH).rearrange("p (k t) -> p k t", k=HB) for _ in range(2)]
        zd = [view(NT * C).rearrange("p (n d) -> p n d", n=NT) for _ in range(2)]
        yd = [v[:, :, :] for v in (xn, x1)]
        s_we = sem("expert_matrices_loaded")
        s_dx = [sem(f"chunk_loaded{q}") for q in range(2)]
        s_g = sem("gates_made")
        s_u = sem("hidden_made")
        s_act = sem("gates_activated")
        s_hid = sem("hidden_multiplied")
        s_hw = sem("hidden_weighted")
        s_ht = sem("hidden_transposed")
        s_hta = sem("hidden_copied_by_scalar")
        s_htv = sem("hidden_copied_by_vector")
        s_yd = sem("down_projected")
        s_zd = sem("residual_added")
        s_vd = sem("chunk_variance_ready")
        s_rd = sem("chunk_rstd_ready")
        s_od = sem("chunk_normalised")
        s_out = [sem(f"chunk_stored{q}") for q in range(2)]
        s_dvd = sem("dve_chain_of_experts")

        block = ctx.enter_context(nc.Block())

        @block.sync
        def _(sp):
            for dst, src in ((wqkv[:, :], w_qkv), (wkvd[QR:QR + KR, 0:2 * P], w_kvdec), (gkv[QR:QR + KR, :], g_kv),
                             (wqd[:, :], w_qdec), (wkr[:, :], w_krope), (wqr[:, :], w_qrope),
                             (wo[:, :], w_o), (rw[:, :], router),
                             (bias_sb[:, :], bias.partition_broadcast(P)),
                             (cos_sb[:, :, :], cos.rearrange("(n p) d -> p n d", p=P)),
                             (sin_sb[:, :, :], sin.rearrange("(n p) d -> p n d", p=P))):
                sp.dma_start(dst, src).then_inc(s_w, 16)

            def attend(b, phase):
                use = scratch_uses(b, phase)
                for item in ITEMS[phase]:
                    kind, d, u, k = item
                    c = b + d
                    if kind == "load_x":
                        after(sp, s_qct, c)
                        sp.dma_start(xn[:, :, :], x[c].rearrange("(n p) d -> p n d", p=P)).then_inc(s_x, 16)
                    elif kind == "load_residual":
                        after(sp, s_x1, NT * c)
                        sp.dma_start(xr[:, :, :], x[c].rearrange("(n p) d -> p n d", p=P)).then_inc(s_xr, 16)
                    elif kind == "stack":
                        if k == 0:
                            if u == 0:
                                n, made = use[("features", 1, NT - 1, 2)]
                                after(sp, s_read[n], made)
                            after(sp, s_exp, SB * c - (SB // 2 if u == 0 else 0))
                        n, part = k // 3, k % 3
                        stack, source = ((ks, (hi, lo, hi)), (qs, (hi, hi, lo)))[n]
                        for i in range(BH):
                            h0, h1, f0, f1 = slots_of(n, i, u)
                            sp.dma_start(stack[part * FD:part * FD + FD, h0:h1:BH, :].bitcast(f32),
                                         source[part][i * FD:i * FD + FD, f0:f1, :].bitcast(f32)).then_inc(s_stk[u], 16)
                    elif kind == "rows":
                        after(sp, s_mh, GROUPS * c + u + 1)
                        after(sp, s_ml, GROUPS * c + u + 1)
                        for n in range(2):
                            sp.dma_start(qs[3 * FD + n:3 * FD + n + 1, HG * u:HG * u + HG, :].bitcast(f32),
                                         rows[:, 0, n, :].bitcast(f32)).then_inc(s_row[u], 16)
                    elif kind == "turn_x1":
                        after(sp, s_x1, NT * c + NT)
                        sp.dma_start(x1_dram[c].rearrange("(n p) d -> p n d", p=P), x1[:, :, :]).then_inc(s_kept, 16)
                    elif kind == "logits":
                        n, made = use[("turn_x1", -1, 0, 0)]
                        after(sp, s_read[n], made)
                        sp.dma_start(x1t_dram[c], x1t[:, :]).then_inc(s_keptt, 16)
                    elif kind == "route" and u == 6:
                        after(sp, s_cw, c + 1)
                        sp.dma_start(cw_dram[c], cw[:, :, :].rearrange("p n e -> p (n e)")).then_inc(s_keptw, 16)

            attend(-1, "before")
            attend(0, "first")
            with sp.Fori(1, B - 1) as b:
                attend(b, "steady")
            attend(B - 1, "last")
            attend(B, "after")
            sp.wait_ge(s_kept, 16 * B)
            sp.wait_ge(s_keptt, 16 * B)
            sp.wait_ge(s_keptw, 16 * B)
            sp.wait_ge(s_pv, GROUPS * B)
            for dst, src in ((wge, gate), (wue, up), (wsh[:, 0:HS], sgate), (wsh[:, HS:], sup),
                             (wdn[:, 0:FE].rearrange("p (k c) -> p k c", c=C), down.rearrange("(k p) c -> p k c", p=P)),
                             (wdn[:, FE:].rearrange("p (k c) -> p k c", c=C), sdown.rearrange("(k p) c -> p k c", p=P))):
                sp.dma_start(dst, src).then_inc(s_we, 16)
            with sp.Fori(0, B // 2) as i:
                for q in range(2):
                    b = 2 * i + q
                    sp.wait_ge(s_u, NT * 2 * i)
                    sp.wait_ge(s_zd, NT * 2 * i)
                    sp.dma_start(xd[q], x1_dram[b].rearrange("(n p) d -> p n d", p=P)).then_inc(s_dx[q], 16)
                    sp.dma_start(xdt[q], x1t_dram[b]).then_inc(s_dx[q], 16)
                    sp.dma_start(cwd[q].rearrange("p n e -> p (n e)"), cw_dram[b]).then_inc(s_dx[q], 16)
                for q in range(2):
                    b = 2 * i + q
                    sp.wait_ge(s_od, NT * b + NT)
                    sp.dma_start(out[b].rearrange("(n p) d -> p n d", p=P), yd[q]).then_inc(s_out[q], 16)
            for q in range(2):
                sp.wait_ge(s_out[q], 16 * (B // 2))

        @block.gpsimd
        def _(pool):
            pool.memset(ident[:, :], 0.0).then_inc(s_zero, 1)
            pool.memset(identb[:, :], 0.0).then_inc(s_zero, 1)
            pool.memset(maskb[:, :], 0.0).then_inc(s_zero, 1)
            pool.memset(lower[:, :, :], 0.0).then_inc(s_zero, 1)
            pool.memset(feat[:, :, 2 * NH:, :], 0.0).then_inc(s_zero, 1)
            pool.memset(ones[:, :], 1.0).then_inc(s_const, 1)
            pool.memset(mhalf[:, :], -0.5).then_inc(s_const, 1)
            pool.wait_ge(s_zero, 5)
            for m in (ident, identb):
                pool.affine_select(out=m[:, :], in_=m[:, :], compare_op=ALU.not_equal, fill=1.0, base=0,
                                   pattern=[[-1, P]], channel_multiplier=1).then_inc(s_const, 1)
            pool.affine_select(out=maskb[:, :], in_=maskb[:, :], compare_op=ALU.is_ge, fill=HIDDEN, base=0,
                               pattern=[[-1, P]], channel_multiplier=1).then_inc(s_const, 1)
            pool.affine_select(out=lower[:, :, :], in_=lower[:, :, :], compare_op=ALU.is_ge, fill=1.0, base=0,
                               pattern=[[-1, E], [1, E]], channel_multiplier=0).then_inc(s_const, 1)

            def attend(b, phase):
                use = scratch_uses(b, phase)
                for item in ITEMS[phase]:
                    kind, d, u, k = item
                    c = b + d
                    if kind == "contents":
                        if u == 0:
                            after(pool, s_va, c)
                        after(pool, s_ms, NT * c + u + 1)
                        pool.tensor_tensor(out=rr[:, u:u + 1], in0=ms[:, u:u + 1], in1=mhalf[:, 0:1],
                                           op=ALU.pow).then_inc(s_rr, 1)
                    elif kind in ("k_rope", "q_rope"):
                        n = kind == "q_rope"
                        bank, made = use[item]
                        after(pool, s_read[bank], made)
                        rope = feat[:, u % 2, NH * n:NH * n + NH, HD:]
                        pool.tensor_tensor(out=rope, in0=rope, in1=turned[n][:, :, :], op=ALU.add).then_inc(s_rope, 1)
                    elif kind == "values":
                        after(pool, s_pv, GROUPS * c)
                        after(pool, s_vn, NT * c + NT)
                        pool.tensor_tensor(out=va[:, :, 0:NH * VW].rearrange("p n (h d) -> p n h d", h=NH)[:, :, :, 0:HD],
                                           in0=vn[:, :, :, :], in1=rr[:, :].unsqueeze(2).unsqueeze(3).to_broadcast([P, NT, NH, HD]),
                                           op=ALU.mult).then_inc(s_va, 1)
                    elif kind == "exp" and k == PS - 1:
                        after(pool, s_msk, 3 * (PAIRS * c + u))
                        after(pool, s_exp, PS * (PAIRS * c + u) + PS)
                        pool.tensor_tensor(out=tick[:, 1:2], in0=mhalf[:, 0:1], in1=mhalf[:, 0:1], op=ALU.add)
                        at = probs[:, (u // 2) % 2, :, :]
                        s = PS * (u % 2)
                        for part in (at[:, s:s + 4, 0:P], at[:, s + 1:s + 4:2, 3 * P:4 * P],
                                     at[:, s + 4, :].rearrange("p (a c) -> p a c", a=2)[:, :, 0:P]):
                            pool.affine_select(out=part, in_=part, compare_op=ALU.is_ge, fill=0.0, base=0,
                                               pattern=[[0, part.shape[1]], [1, P]],
                                               channel_multiplier=-1).then_inc(s_msk, 1)
                    elif kind == "x1":
                        after(pool, s_var, c + 1)
                        pool.tensor_tensor(out=rstd[:, :], in0=ve[:, :], in1=mhalf[:, :], op=ALU.pow).then_inc(s_rstd, 1)

            attend(-1, "before")
            attend(0, "first")
            with pool.Fori(1, B - 1) as b:
                attend(b, "steady")
            attend(B - 1, "last")
            attend(B, "after")
            with pool.Fori(0, B // 2) as i:
                for q in range(2):
                    pool.wait_ge(s_dx[q], 48 * i + 48)
                    for t in range(NT):
                        n = NT * (2 * i + q) + t
                        pool.wait_ge(s_hid, 2 * n + 2)
                        h = hid[t % 2][:, 0:FE].rearrange("p (e k) -> p e k", e=E)
                        pool.tensor_tensor(out=h, in0=h, in1=cwd[q][:, t, :].unsqueeze(2).to_broadcast([P, E, HE]),
                                           op=ALU.mult).then_inc(s_hw, 1)
                    pool.wait_ge(s_vd, 2 * i + q + 1)
                    pool.tensor_tensor(out=rstd[:, :], in0=ve[:, :], in1=mhalf[:, :], op=ALU.pow).then_inc(s_rd, 1)

        @block.scalar
        def _(act):
            act.wait_ge(s_const, CONSTS)

            def attend(b, phase):
                use = scratch_uses(b, phase)
                for item in ITEMS[phase]:
                    kind, d, u, k = item
                    c = b + d
                    if item in use:
                        n, made = use[item]
                        bank = psum[:, SCRATCH_BANKS[n], :]
                    if kind == "turn_x":
                        after(act, s_made[n], made)
                        act.activation(xt[:, :], bank, ACT.Copy).then_inc(s_read[n], 1)
                    elif kind == "latents":
                        after(act, s_made[n], made)
                        act.activation(qct[:, :], bank[0:QR + KR, :], ACT.Copy).then_inc(s_qct, 1)
                        act.activation(sq[:, :], bank[0:QR + KR, :], ACT.Square).then_inc(s_read[n], 1)
                    elif kind == "contents":
                        after(act, s_va, c)
                        after(act, s_rr, NT * c + u + 1)
                        parts = bank[:, 0:3 * P].rearrange("p (n h d) -> p n h d", n=3, h=NH)
                        act.activation(vn[:, u, :, :], parts[:, 2, :, :], ACT.Copy).then_inc(s_vn, 1)
                        act.activation(feat[:, u % 2, NH:2 * NH, 0:HD], parts[:, 0, :, :], ACT.Copy)
                        act.activation(feat[:, u % 2, 0:NH, 0:HD], parts[:, 1, :, :], ACT.Copy,
                                       scale=rr[:, u:u + 1]).then_inc(s_read[n], 1)
                    elif kind == "features":
                        if u == 0 and k == 0:
                            for half in range(HALVES):
                                after(act, s_stk[half], STACKED * c)
                        after(act, s_made[n], made)
                        f0, f1 = 4 * k, min(4 * k + 4, FB)
                        act.activation(hi[0:FR, f0:f1, u * P:u * P + P],
                                       bank[0:FR, 0:(f1 - f0) * P].rearrange("p (f t) -> p f t", t=P),
                                       ACT.Copy).then_inc(s_hi, 1)
                    elif kind == "exp":
                        m = PS * u + k
                        if m % (2 * PS) == 0:
                            after(act, s_pv, GROUPS * c + u // 2 - 1)
                        after(act, s_st, SB * c + m + 1)
                        act.activation(probs[:, (u // 2) % 2, PS * (u % 2) + k, :], psum[:, 4 + m % 2, :], ACT.Exp,
                                       scale=SCALE).then_inc(s_exp, 1)
                    elif kind == "rows":
                        after(act, s_row[(u - 1) % GROUPS], 32 * c + 32 if u else 32 * c)
                        after(act, s_nmt, GROUPS * c + u + 1)
                        act.activation(rows[:, 0, 0, :], psum[0:HG, 7, :], ACT.Copy).then_inc(s_mh, 1)
                    elif kind == "pv":
                        after(act, s_otr, GROUPS * c + u)
                        after(act, s_pv, GROUPS * c + u + 1)
                        act.activation(ot[:, :], psum[:, 6, :], ACT.Copy).then_inc(s_oc, 1)
                    elif kind == "turn_heads":
                        after(act, s_keptt, 16 * c)
                        after(act, s_made[n], made)
                        act.activation(ont[:, :], bank, ACT.Copy).then_inc(s_read[n], 1)
                    elif kind == "turn_x1":
                        after(act, s_made[n], made)
                        act.activation(x1t[:, :], bank, ACT.Copy).then_inc(s_read[n], 1)
                    elif kind == "logits":
                        after(act, s_cw, c)
                        after(act, s_made[n], made)
                        act.activation(sc[:, :, :], bank[:, 0:NT * E].rearrange("p (n e) -> p n e", n=NT), ACT.Exp,
                                       scale=-1.0).then_inc(s_read[n], 1)

            attend(-1, "before")
            attend(0, "first")
            with act.Fori(1, B - 1) as b:
                attend(b, "steady")
            attend(B - 1, "last")
            attend(B, "after")

            def copy_hidden(n, t):
                act.wait_ge(s_ht, n + 1)
                act.activation(hidt[t % 2][:, 0:4, :], psum[:, 6, :].rearrange("p (k t) -> p k t", k=4),
                               ACT.Copy).then_inc(s_hta, 1)

            with act.Fori(0, B // 2) as i:
                for m in range(2 * NT):
                    n = 2 * NT * i + m
                    p = m % 2
                    act.wait_ge(s_g, n + 1)
                    act.wait_ge(s_hid, 2 * (n - 1) if m >= 2 else 2 * NT * 2 * i)
                    act.activation(act_out[p][:, 0:FE], psum[:, 3 * p, :], ACT.Silu).then_inc(s_act, 1)
                    if m:
                        copy_hidden(n - 1, m - 1)
                    act.wait_ge(s_u, n + 1)
                    act.activation(act_out[p][:, FE:FH], psum[:, 3 * p + 2, 0:HS], ACT.Silu).then_inc(s_act, 1)
                copy_hidden(2 * NT * i + 2 * NT - 1, 2 * NT - 1)

        @block.vector
        def _(dve):
            dve.memset(ks[96:P, :, :].bitcast(f32), 1.0).then_inc(s_const, 1)
            dve.memset(va[:, :, :], 1.0).then_inc(s_const, 1)
            dve.wait_ge(s_w, 16 * 11)
            dve.tensor_scalar(wkvg[QR:QR + KR, :], wkvd[QR:QR + KR, 0:2 * P], gkv[QR:QR + KR, 0:1], None,
                              ALU.mult).then_inc(s_const, 1)
            LINKS = 37

            def attend(b, phase):
                use = scratch_uses(b, phase)
                linked = [0]

                def link(ins):
                    linked[0] += 1
                    ins.then_inc(s_dve, 1)
                    after(dve, s_dve, LINKS * (b - 1) + linked[0])

                def ranks(out_, mine, other, gt, eq, low):
                    dve.tensor_tensor(gt, other, mine, ALU.is_gt)
                    link(dve.tensor_tensor(eq, other, mine, ALU.is_equal))
                    link(dve.tensor_tensor(eq, eq, low, ALU.mult))
                    link(dve.tensor_tensor(gt, gt, eq, ALU.add))
                    link(dve.tensor_reduce(out_, gt, AX.X, ALU.add))

                for item in ITEMS[phase]:
                    kind, d, u, k = item
                    c = b + d
                    if item in use:
                        n, made = use[item]
                        bank = psum[:, SCRATCH_BANKS[n], :]
                    if kind in ("k_rope", "q_rope"):
                        which = kind == "q_rope"
                        after(dve, s_rope, 2 * (NT * c + u - 1) + which + 1)
                        after(dve, s_made[n], made)
                        src = bank.rearrange("p (h d) -> p h d", h=NH)
                        H = RD // 2
                        dve.tensor_tensor(feat[:, u % 2, NH * which:NH * which + NH, HD:], src,
                                          cos_sb[:, u, :].unsqueeze(1).to_broadcast([P, NH, RD]), ALU.mult)
                        for a_, c_ in ((0, H), (H, 0)):
                            a = dve.tensor_tensor(turned[which][:, :, a_:a_ + H], src[:, :, c_:c_ + H],
                                                  sin_sb[:, u, a_:a_ + H].unsqueeze(1).to_broadcast([P, NH, H]), ALU.mult)
                        a.then_inc(s_read[n], 1)
                    elif kind == "contents":
                        after(dve, s_made[n], made)
                        dve.tensor_scalar(ms[:, u:u + 1], bank[:, 3 * P:3 * P + 1], 1.0 / KR, RMS_EPS,
                                          ALU.mult, ALU.add).then_inc(s_ms, 1)
                    elif kind == "features":
                        after(dve, s_hi, 3 * (NT * c + u) + k + 1)
                        f0, f1 = 4 * k, min(4 * k + 4, FB)
                        dve.tensor_tensor(lo[0:FR, f0:f1, u * P:u * P + P],
                                          bank[0:FR, 0:(f1 - f0) * P].rearrange("p (f t) -> p f t", t=P),
                                          hi[0:FR, f0:f1, u * P:u * P + P].bitcast(f32), ALU.subtract).then_inc(s_read[n], 1)
                    elif kind == "max":
                        m = PS * u + k
                        g = u // 2
                        if m % (2 * PS) == 0:
                            after(dve, s_nmt, GROUPS * c + g - 1)
                        after(dve, s_mx, SB * c + m + 1)
                        if k == PS - 1:
                            a = dve.tensor_reduce(nm[:, g % 2, 1, 2 * (u % 2):2 * (u % 2) + 2],
                                                  psum[:, m % 2, :].rearrange("p (a c) -> p a c", a=2), AX.X, ALU.max, negate=True)
                        else:
                            for i, qt, c0 in MAX_STEPS[k]:
                                h = 2 * (u % 2) + i
                                a = dve.tensor_reduce(nm[:, g % 2, qt, h:h + 1], psum[:, m % 2, c0:c0 + (qt + 1) * P],
                                                      AX.X, ALU.max, negate=True)
                        a.then_inc(s_mxr, 1)
                    elif kind == "rows":
                        after(dve, s_mh, GROUPS * c + u + 1)
                        dve.tensor_tensor(rows[:, 0, 1, :], psum[0:HG, 7, :], rows[:, 0, 0, :].bitcast(f32),
                                          ALU.subtract).then_inc(s_ml, 1)
                    elif kind == "turn":
                        after(dve, s_otr, GROUPS * c + u + 1)
                        heads = psum[:, 7, :].rearrange("p (n h c) -> p n h c", n=NT, h=HG)
                        dve.reciprocal(rs[:, :, :].unsqueeze(3), heads[:, :, :, HD:HD + 1]).then_inc(s_rs, 1)
                        after(dve, s_rs, GROUPS * c + u + 1)
                        dve.tensor_tensor(on[:, :, HG * u:HG * u + HG, :], heads[:, :, :, 0:HD],
                                          rs[:, :, :].unsqueeze(3).to_broadcast([P, NT, HG, HD]),
                                          ALU.mult).then_inc(s_on, 1)
                    elif kind == "project_out":
                        after(dve, s_xr, 16 * c + 16)
                        after(dve, s_made[n], made)
                        dve.tensor_tensor(z[:, :, :], bank.rearrange("p (n d) -> p n d", n=NT), xr[:, :, :],
                                          ALU.add).then_inc(s_read[n], 1)
                        after(dve, s_read[n], made)
                        for t in range(NT):
                            a = dve.bn_stats(st6[:, t, :], z[:, t, :])
                        link(a)
                        dve.tensor_copy(tick[:, 0:1], mhalf[:, 0:1])
                        for t in range(NT):
                            a = dve.bn_aggr(mv[:, t, :], st6[:, t, :])
                        link(a)
                        dve.tensor_scalar(ve[:, :].unsqueeze(2), mv[:, :, 1:2], LN_EPS, None, ALU.add).then_inc(s_var, 1)
                    elif kind == "x1":
                        after(dve, s_rstd, c + 1)
                        after(dve, s_kept, 16 * c)
                        for t in range(NT):
                            dve.tensor_scalar(x1[:, t, :], z[:, t, :], mv[:, t, 0:1], rstd[:, t:t + 1], ALU.subtract,
                                              ALU.mult).then_inc(s_x1, 1)
                    elif kind == "route" and u == 0:
                        n, made = use[("logits", -1, 0, 0)]
                        after(dve, s_read[n], made)
                        link(dve.tensor_scalar(sc[:, :, :], sc[:, :, :], 1.0, None, ALU.add))
                        link(dve.reciprocal(sc[:, :, :], sc[:, :, :]))
                        link(dve.tensor_tensor(sbias[:, :, :], sc[:, :, :],
                                               bias_sb[:, :].unsqueeze(1).to_broadcast([P, NT, E]), ALU.add))
                        four = sbias[:, :, :].rearrange("p n (g e) -> p (n g) e", g=NG)
                        a0, a1, a2, a3 = (four[:, :, i:i + 1] for i in range(EG))
                        s0, s1, s2, s3, s4, s5 = (t2[:, i, :].unsqueeze(2) for i in range(6))
                        dve.tensor_tensor(s0, a0, a1, ALU.max)
                        dve.tensor_tensor(s1, a0, a1, ALU.min)
                        dve.tensor_tensor(s2, a2, a3, ALU.max)
                        link(dve.tensor_tensor(s3, a2, a3, ALU.min))
                        dve.tensor_tensor(s4, s0, s2, ALU.min)
                        link(dve.tensor_tensor(s5, s1, s3, ALU.max))
                        link(dve.tensor_tensor(s1, s0, s2, ALU.max))
                        link(dve.tensor_tensor(s3, s4, s5, ALU.max))
                        link(dve.tensor_tensor(s0, s1, s3, ALU.add))
                    elif kind == "route" and u == 1:
                        gs = t2[:, 0, :].rearrange("p (n g) -> p n g", n=NT)
                        NG2 = [P, NT, NG, NG]
                        gt, eq = (v[:, 0:NG, :].rearrange("p n (g f) -> p n g f", g=NG) for v in (above, equal))
                        ranks(gmask[:, :, :], gs.unsqueeze(3).to_broadcast(NG2), gs.unsqueeze(2).to_broadcast(NG2),
                              gt, eq, lower[:, 0:NG, 0:NG].unsqueeze(1).to_broadcast(NG2))
                        link(dve.tensor_scalar(gmask[:, :, :], gmask[:, :, :], TOPG - 0.5, -3e38, ALU.is_gt, ALU.mult))
                        link(dve.tensor_tensor(masked[:, :, :].rearrange("p n (g e) -> p (n g) e", g=NG),
                                               sbias[:, :, :].rearrange("p n (g e) -> p (n g) e", g=NG),
                                               gmask[:, :, :].rearrange("p n g -> p (n g)").unsqueeze(2).to_broadcast([P, NT * NG, EG]),
                                               ALU.add))
                    elif kind == "route" and u < 6:
                        v = masked[:, u - 2, :]
                        ranks(rank[:, u - 2, :], v.unsqueeze(2).to_broadcast([P, E, E]), v.unsqueeze(1).to_broadcast([P, E, E]),
                              above[:, :, :], equal[:, :, :], lower[:, :, :])
                    elif kind == "route":
                        link(dve.tensor_scalar(rank[:, :, :], rank[:, :, :], TOPK - 0.5, None, ALU.is_lt))
                        link(dve.tensor_tensor(rank[:, :, :], rank[:, :, :], sc[:, :, :], ALU.mult))
                        link(dve.tensor_reduce(wsum[:, 0, :], rank[:, :, :], AX.X, ALU.add))
                        link(dve.tensor_scalar(wsum[:, 0, :], wsum[:, 0, :], 1e-20, None, ALU.add))
                        link(dve.reciprocal(wsum[:, 1, :], wsum[:, 0, :]))
                        after(dve, s_keptw, 16 * c)
                        dve.tensor_tensor(cw[:, :, :], rank[:, :, :], wsum[:, 1, :].unsqueeze(2).to_broadcast([P, NT, E]),
                                          ALU.mult).then_inc(s_cw, 1)
                assert linked[0] in (0, LINKS)

            attend(-1, "before")
            attend(0, "first")
            with dve.Fori(1, B - 1) as b:
                attend(b, "steady")
            attend(B - 1, "last")
            attend(B, "after")

            DLINKS = 4
            with dve.Fori(0, B // 2) as i:
                linkd = [0]

                def linkx(ins):
                    linkd[0] += 1
                    ins.then_inc(s_dvd, 1)
                    dve.wait_ge(s_dvd, DLINKS * i + linkd[0])

                def down_out(m):
                    n, q, t = 2 * NT * i + m, m // NT, m % NT
                    dve.wait_ge(s_ht, n + 1)
                    dve.tensor_copy(hidt[m % 2][:, 4:HB, :],
                                    psum[:, 7, 0:HS].rearrange("p (k t) -> p k t", k=HB - 4)).then_inc(s_htv, 1)
                    dve.wait_ge(s_yd, n + 1)
                    dve.tensor_tensor(zd[q][:, t, :], psum[:, 7, HS:HS + C], xd[q][:, t, :], ALU.add).then_inc(s_zd, 1)

                def norm(q):
                    b = 2 * i + q
                    dve.wait_ge(s_zd, NT * b + NT)
                    for t in range(NT):
                        a = dve.bn_stats(st6[:, t, :], zd[q][:, t, :])
                    linkx(a)
                    dve.tensor_copy(tick[:, 0:1], mhalf[:, 0:1])
                    for t in range(NT):
                        a = dve.bn_aggr(mv[:, t, :], st6[:, t, :])
                    linkx(a)
                    dve.tensor_scalar(ve[:, :].unsqueeze(2), mv[:, :, 1:2], LN_EPS, None, ALU.add).then_inc(s_vd, 1)
                    dve.wait_ge(s_rd, b + 1)
                    dve.wait_ge(s_out[q], 16 * i)
                    for t in range(NT):
                        dve.tensor_scalar(yd[q][:, t, :], zd[q][:, t, :], mv[:, t, 0:1], rstd[:, t:t + 1],
                                          ALU.subtract, ALU.mult).then_inc(s_od, 1)

                for m in range(2 * NT):
                    n, p = 2 * NT * i + m, m % 2
                    if m % NT == 0:
                        dve.wait_ge(s_dx[m // NT], 48 * i + 48)
                    if m:
                        down_out(m - 1)
                    dve.wait_ge(s_ht, n - 1 if m >= 2 else 2 * NT * i)
                    for c in range(2):
                        dve.wait_ge(s_act, 2 * n + c + 1)
                        dve.wait_ge(s_u, n + 1)
                        a, b_, src = ((0, FE, psum[:, 3 * p + 1, :]), (FE, FH, psum[:, 3 * p + 2, HS:]))[c]
                        dve.tensor_tensor(hid[p][:, a:b_], src, act_out[p][:, a:b_], ALU.mult).then_inc(s_hid, 1)
                    if m == NT:
                        norm(0)
                down_out(2 * NT - 1)
                norm(1)
                assert linkd[0] == DLINKS

        @block.tensor
        def _(pe):
            pe.wait_ge(s_w, 16 * 11)
            pe.wait_ge(s_const, CONSTS)

            def attend(b, phase):
                use = scratch_uses(b, phase)

                def wait_use(item):
                    after(pe, s_read[use[item][0]], use[item][1])

                for item in ITEMS[phase]:
                    kind, d, u, k = item
                    c = b + d
                    at = slice(u * P, u * P + P)
                    if item in use:
                        n, made = use[item]
                        bank = psum[:, SCRATCH_BANKS[n], :]
                        after(pe, s_read[n], made - 1)
                    if kind == "turn_x":
                        after(pe, s_x, 16 * c + 16)
                        for t in range(NT):
                            a = pe.transpose(bank[:, t * P:t * P + P], xn[:, t, :], ident[:, :])
                        a.then_inc(s_made[n], 1)
                    elif kind == "latents":
                        wait_use(("turn_x", d, 0, 0))
                        pe.matmul(bank[0:QR + KR, :], wqkv[:, :], xt[:, :], start=True, stop=True).then_inc(s_made[n], 1)
                    elif kind == "k_rope":
                        pe.matmul(bank, xt[:, at], wkr[:, :], start=True, stop=True).then_inc(s_made[n], 1)
                    elif kind == "q_rope":
                        if u == 0:
                            wait_use(("latents", d, 0, 0))
                        pe.matmul(bank, qct[0:QR, at], wqr[:, :], start=True, stop=True).then_inc(s_made[n], 1)
                    elif kind == "contents":
                        pe.matmul(bank[:, 0:P], qct[0:QR, at], wqd[:, :], start=True, stop=True)
                        pe.matmul(bank[:, P:3 * P], qct[QR:QR + KR, at], wkvg[QR:QR + KR, :], start=True, stop=True)
                        pe.matmul(bank[:, 3 * P:3 * P + 1], sq[QR:QR + KR, at], ones[QR:QR + KR, :],
                                  start=True, stop=True).then_inc(s_made[n], 1)
                    elif kind == "features":
                        if k == 0:
                            after(pe, s_rope, 2 * (NT * c + u) + 2)
                            wait_use(("contents", d, u, 0))
                        tile = feat[:, u % 2, :, :].rearrange("p s d -> p (s d)")
                        for f in range(4 * k, min(4 * k + 4, FB)):
                            a = pe.transpose(bank[0:FR, (f - 4 * k) * P:(f - 4 * k) * P + P],
                                             tile[:, f * FR:f * FR + FR], ident[:, :])
                        a.then_inc(s_made[n], 1)
                    elif kind == "max":
                        m = PS * u + k
                        if m % (SB // HALVES) == 0:
                            half = m // (SB // HALVES)
                            after(pe, s_stk[half], STACKED * c + STACKED)
                        after(pe, s_mxr, SB * c + m - 1)
                        for i, qt, c0 in MAX_STEPS[k]:
                            w = (qt + 1) * P
                            dst = psum[:, m % 2, c0:c0 + w]
                            pe.matmul(dst, qs[0:3 * FD, 2 * u + i, qt * P:qt * P + P],
                                      ks[0:3 * FD, 2 * u + i, 0:w], start=True, stop=False)
                            a = pe.matmul(dst[:, w - P:w], identb[:, :], maskb[:, :], start=False, stop=True)
                        a.then_inc(s_mx, 1)
                    elif kind == "rows":
                        after(pe, s_mxr, SB * c + 2 * PS * (u + 1))
                        after(pe, s_ml, GROUPS * c + u)
                        after(pe, s_on, GROUPS * c + u - 1)
                        for qt in range(NT):
                            a = pe.matmul(psum[0:HG, 7, qt * P:qt * P + P], nm[:, u % 2, qt, :], ident[:, :],
                                          start=True, stop=True)
                        a.then_inc(s_nmt, 1)
                    elif kind == "exp":
                        m = PS * u + k
                        if m % (2 * PS) == 0:
                            after(pe, s_row[u // 2], 32 * c + 32)
                        after(pe, s_exp, SB * c + m - 1)
                        for i, kt, c0 in EXP_STEPS[k]:
                            h = 2 * u + i
                            w = T - kt * P
                            a = pe.matmul(psum[:, 4 + m % 2, c0:c0 + w], ks[0:3 * FD + 2, h, kt * P:kt * P + P],
                                          qs[0:3 * FD + 2, h, kt * P:T], start=True, stop=True)
                        a.then_inc(s_st, 1)
                    elif kind == "pv":
                        if u == 0:
                            after(pe, s_va, c + 1)
                        after(pe, s_msk, 6 * (GROUPS * c + u) + 6)
                        after(pe, s_oc, GROUPS * c + u)
                        for kt in range(NT):
                            for j in range(HG):
                                i, s = j % 2, PS * (j // 2)
                                slot, c0 = ((s + 4, 2 * P * i) if kt == 2 else
                                            (s + 2 * i + (kt > 0), 3 * P if kt == 3 else 0))
                                w = T - kt * P
                                h = HG * u + j
                                a = pe.matmul(psum[SLOT * j:SLOT * j + SLOT, 6, kt * P:T], va[:, kt, h * VW:h * VW + SLOT],
                                              probs[:, u % 2, slot, c0:c0 + w], start=kt == 0, stop=kt == NT - 1)
                        a.then_inc(s_pv, 1)
                    elif kind == "turn":
                        after(pe, s_oc, GROUPS * c + u + 1)
                        after(pe, s_ml, GROUPS * c + u + 2 if phase != "after" else GROUPS * B)
                        after(pe, s_on, GROUPS * c + u)
                        for qt in range(NT):
                            a = pe.transpose(psum[:, 7, qt * P:qt * P + P], ot[:, qt * P:qt * P + P], ident[:, :])
                        a.then_inc(s_otr, 1)
                    elif kind == "turn_heads":
                        after(pe, s_on, GROUPS * c + GROUPS)
                        for t in range(NT):
                            a = pe.transpose(bank[:, t * P:t * P + P], on[:, t, :, :].rearrange("p h d -> p (h d)"), ident[:, :])
                        a.then_inc(s_made[n], 1)
                    elif kind == "project_out":
                        wait_use(("turn_heads", d, 0, 0))
                        for t in range(NT):
                            a = pe.matmul(bank[:, t * P:t * P + P], ont[:, t * P:t * P + P], wo[:, :], start=True, stop=True)
                        a.then_inc(s_made[n], 1)
                    elif kind == "turn_x1":
                        after(pe, s_x1, NT * c + NT)
                        for t in range(NT):
                            a = pe.transpose(bank[:, t * P:t * P + P], x1[:, t, :], ident[:, :])
                        a.then_inc(s_made[n], 1)
                    elif kind == "logits":
                        wait_use(("turn_x1", d, 0, 0))
                        for t in range(NT):
                            a = pe.matmul(bank[:, t * E:t * E + E], x1t[:, t * P:t * P + P], rw[:, :], start=True, stop=True)
                        a.then_inc(s_made[n], 1)

            attend(-1, "before")
            attend(0, "first")
            with pe.Fori(1, B - 1) as b:
                attend(b, "steady")
            attend(B - 1, "last")
            attend(B, "after")

            pe.wait_ge(s_we, 16 * 6)
            pe.wait_ge(s_mxr, SB * B)
            pe.wait_ge(s_exp, SB * B)
            pe.wait_ge(s_on, GROUPS * B)
            pe.wait_ge(s_cw, B)

            def gates(i, m):
                q, t, p = m // NT, m % NT, m % 2
                if t == 0:
                    pe.wait_ge(s_dx[q], 48 * i + 48)
                pe.wait_ge(s_hid, 2 * (2 * NT * i + m - 1) if m >= 2 else 2 * 2 * NT * i)
                pe.matmul(psum[:, 3 * p, :], xdt[q][:, t * P:t * P + P], wge, start=True, stop=True).then_inc(s_g, 1)

            def ups(m):
                q, t, p = m // NT, m % NT, m % 2
                pe.matmul(psum[:, 3 * p + 1, :], xdt[q][:, t * P:t * P + P], wue, start=True, stop=True)
                pe.matmul(psum[:, 3 * p + 2, :], xdt[q][:, t * P:t * P + P], wsh, start=True, stop=True).then_inc(s_u, 1)

            with pe.Fori(0, B // 2) as i:
                gates(i, 0)
                ups(0)
                for m in range(2 * NT):
                    n, p = 2 * NT * i + m, m % 2
                    pe.wait_ge(s_hw, n + 1)
                    pe.wait_ge(s_hta, n)
                    pe.wait_ge(s_zd, n)
                    for k in range(HB):
                        a = pe.transpose(psum[:, 6 + k // 4, (k % 4) * P:(k % 4) * P + P],
                                         hid[p][:, k * P:k * P + P], ident[:, :])
                    a.then_inc(s_ht, 1)
                    if m + 1 < 2 * NT:
                        gates(i, m + 1)
                    pe.wait_ge(s_hta, n + 1)
                    pe.wait_ge(s_htv, n + 1)
                    for k in range(HB):
                        a = pe.matmul(psum[:, 7, HS:HS + C], hidt[p][:, k, :], wdn[:, k * C:k * C + C],
                                      start=k == 0, stop=k == HB - 1)
                    a.then_inc(s_yd, 1)
                    if m + 1 < 2 * NT:
                        ups(m + 1)


def kernel(**inputs):
    import numpy as _np
    import concourse.bacc as _bacc
    from concourse import mybir as _mybir
    from concourse.bass_utils import run_bass_kernel_spmd as _run

    f = {k.split("_", 2)[2]: _np.asarray(v) for k, v in inputs.items() if k.startswith("L0_ffn")}
    a = {k.split("_", 2)[2]: _np.asarray(v) for k, v in inputs.items() if k.startswith("L0_attn")}

    inv_freq = 1.0 / 10000.0 ** (_np.arange(0, RD, 2, dtype=_np.float32) / RD)
    freqs = _np.outer(_np.arange(T, dtype=_np.float32), inv_freq)
    emb = _np.concatenate([freqs, freqs], -1)
    sign = _np.where(_np.arange(RD) < RD // 2, -1.0, 1.0)
    arrays = {
        "x": a["x"],
        "w_qkv": _np.concatenate([a["W_q"], a["W_kv"]], 1),
        "w_kvdec": _np.concatenate([a["W_kdec"], a["W_vdec"]], 1),
        "g_kv": a["g_kv"].reshape(KR, 1),
        "w_qdec": a["W_qdec"],
        "w_krope": a["W_krope"],
        "w_qrope": a["W_qrope"],
        "w_o": a["W_o"],
        "router": f["router_w"].T,
        "bias": f["correction_bias"],
        "gate": f["gate_w"].transpose(1, 0, 2).reshape(C, E * HE),
        "up": f["up_w"].transpose(1, 0, 2).reshape(C, E * HE),
        "down": f["down_w"].reshape(E * HE, C),
        "sgate": f["shared_gate_w"].T,
        "sup": f["shared_up_w"].T,
        "sdown": f["shared_down_w"].T,
        "cos": _np.cos(emb).astype(_np.float32),
        "sin": (_np.sin(emb) * sign).astype(_np.float32),
    }
    nc = _bacc.Bacc("TRN2", target_bir_lowering=False, num_devices=1)
    f32 = _mybir.dt.float32
    sent, args = {}, []
    for name, v in arrays.items():
        sent["in_" + name] = _np.ascontiguousarray(v)
        args.append(nc.dram_tensor("in_" + name, v.shape, f32, kind="ExternalInput").ap())
    args.append(nc.dram_tensor("out_0", (B, T, C), f32, kind="ExternalOutput").ap())
    args.append(nc.dram_tensor("x1_kept", (B, T, C), f32, kind="Internal").ap())
    args.append(nc.dram_tensor("x1t_kept", (B, C, T), f32, kind="Internal").ap())
    args.append(nc.dram_tensor("weights_kept", (B, P, NT * E), f32, kind="Internal").ap())
    mla_moe_kernel(nc, *args)
    r = _run(nc, [sent], core_ids=[0])
    return r.results[0]["out_0"]
```

```python
import concourse.bass as bass
from concourse import mybir
from contextlib import ExitStack

B, T, C = 16, 512, 128
NH, HD, RD = 16, 8, 32
FD = HD + RD
QR, KR = 64, 32
E, NG, HE = 16, 4, 32
EG = E // NG
TOPG, TOPK = 2, 4
HS = 256
P = 128
NT = T // P
RMS_EPS, LN_EPS = 1e-6, 1e-5
BH = P // FD
FR = BH * FD
SLOTS = (2 * NH + BH - 1) // BH * BH
FB = SLOTS // BH
HG = 4
GROUPS = NH // HG
PAIRS = NH // 2
SCALE = 1.0 / float(FD) ** 0.5
HIDDEN = -1e30
SLOT = 32
VW = HD + 1
PS = 5

MAX_STEPS = (((0, 3, 0),), ((0, 2, 0), (0, 0, 384)), ((1, 3, 0),), ((1, 2, 0), (1, 0, 384)),
             ((0, 1, 0), (1, 1, 256)))
EXP_STEPS = (((0, 0, 0),), ((0, 1, 0), (0, 3, 384)), ((1, 0, 0),), ((1, 1, 0), (1, 3, 384)),
             ((0, 2, 0), (1, 2, 256)))
SB = PS * PAIRS
SHARES = ((0, 3), (3, 6), (6, 8))
PARTS = 3
FT = 3
STACK_STEPS = ((18, 18, 22, 24, 24, 25), (30, 32, 33, 34, 34, 37), (41, 43, 45, 45, 46, 46))
X_STEPS = (1, 18, 20)
VALUES_STEP = 1
TILE_STEPS = ((20, 25, 1, (4, 6, 7)), (25, 26, 2, (8, 11, 12)), (30, 36, 4, (13, 15, 15)), (54, 54, 13, (16, 16, 17)))
PV_LAG, TURN_LAG = 11, 13
ROWS_LEAD = 4
OUT_STEPS = (6, 10, 11, 25, 26)
ROUTE_STEPS = (0, 1, 1, 2, 5, 6, 19)
AHEAD = 13


def steady_steps():
    at = [[] for _ in range(SB)]

    def put(step, *item):
        at[step].append(item)

    put(0, "load_residual", -1, 0, 0)
    for share, steps in enumerate(STACK_STEPS):
        for n, step in enumerate(steps):
            put(step % SB, "stack", int(step < SB), share, n)
    put(X_STEPS[0], "load_x", 2, 0, 0)
    put(X_STEPS[1], "turn_x", 2, 0, 0)
    put(X_STEPS[2], "latents", 2, 0, 0)
    put(VALUES_STEP, "values", 0, 0, 0)
    for t, (k, q, c, f) in enumerate(TILE_STEPS):
        put(k % SB, "k_rope", 2 if k < SB else 1, t, 0)
        put(q % SB, "q_rope", 2 if q < SB else 1, t, 0)
        put(c, "contents", 1, t, 0)
        for n in range(3):
            put(f[n], "features", 1, t, n)
    for g in range(GROUPS):
        for name, lag in (("pv", PV_LAG), ("turn", TURN_LAG)):
            put((2 * PS * g + lag) % SB, name, 0 if 2 * PS * g + lag < SB else -1, g, 0)
        put((2 * PS * g - ROWS_LEAD) % SB, "rows", 0 if g else 1, g, 0)
    for name, step in zip(("turn_heads", "project_out", "x1", "turn_x1", "logits"), OUT_STEPS):
        put(step, name, -1, 0, 0)
    for n, step in enumerate(ROUTE_STEPS):
        put(step, "route", -2, n, 0)
    steps = []
    for n in range(SB):
        m = n + AHEAD
        steps.append(("max", m // SB, m % SB // PS, m % PS))
        steps += at[n]
        steps.append(("exp", 0, n // PS, n % PS))
    return steps


STEADY = steady_steps()
PHASES = {"before2": (2,), "before": (1, 2), "first": (0, 1, 2), "second": (-1, 0, 1, 2), "steady": (-2, -1, 0, 1, 2),
          "last2": (-2, -1, 0, 1), "last": (-2, -1, 0), "after": (-1,), "after2": (-2,)}
ITEMS = {phase: [item for item in STEADY if item[1] in batches] for phase, batches in PHASES.items()}


def with_routing(items):
    routing = [("route", -1) + item[2:] for item in STEADY if item[0] == "route"]
    found = []
    for item in items:
        found.append(item)
        if item[0] == "exp" and PS * item[2] + item[3] > OUT_STEPS[-1] and routing:
            found.append(routing.pop(0))
    return found + routing


ITEMS["last"] = with_routing(ITEMS["last"])
SCRATCH = ("turn_x", "latents", "k_rope", "q_rope", "contents", "features", "turn_heads",
           "project_out", "turn_x1", "logits")
SCRATCH_BANKS = (2, 3)


def scratch_uses(b, phase):
    def uses(p):
        return [item for item in ITEMS[p] if item[0] in SCRATCH]

    start = 0
    for p in PHASES:
        if p == phase:
            if p == "steady":
                start = len(uses(p)) // 2 * (b - 2) + start
            break
        start += len(uses(p)) // 2 * (B - 4 if p == "steady" else 1)
    return {"start": start} | {item: (n % 2, start + (n // 2 + 1)) for n, item in enumerate(uses(phase))}


MAX_BANKS = (0, 1, 6)
MAX_FREE = {m % 3: m + 1 - SB for m in range(SB - 3, SB)}
SCRATCH_END = sum(sum(item[0] in SCRATCH for item in ITEMS[p]) // 2 * (B - 4 if p == "steady" else 1) for p in PHASES)


def slots_of(n, i, share):
    u0, u1 = SHARES[share]
    heads = [h for h in range(2 * u0, 2 * u1) if (n * NH + h) % BH == i]
    return heads[0], heads[-1] + 1, (n * NH + heads[0]) // BH, (n * NH + heads[-1]) // BH + 1


STACKED = 16 * PARTS * BH
FE = E * HE
FH = FE + HS
HB = FH // P
ROUTING_AT = 1
ROUTED = FE // P


def chunk_items():
    items = []
    for n, block in enumerate([*range(ROUTED, HB), *range(ROUTED)]):
        items.append(("hidden", n, block))
        if 1 <= n <= NT:
            items.append(("down", n - 1, 0))
        if n == 2:
            items.append(("out", 0, 0))
        if n == 3:
            items.append(("split", 0, 0))
    items += [("weights", 0, 0), ("norm", 0, 0)]
    return items


CHUNK_ITEMS = chunk_items()


def last_routing(c, n):
    at = HB * c + n - ROUTING_AT if isinstance(c, int) else -1
    return slice(at, at + 1) if 0 <= at < len(ITEMS["after2"]) else None


def count_of(c):
    return c // 2 + 1


def within(c, first, end):
    return not isinstance(c, int) or first <= c < end


def after(engine, semaphore, value):
    if not isinstance(value, int) or value > 0:
        engine.wait_ge(semaphore, value)


def mla_moe_kernel(nc, x, w_qkv, w_kvdec, g_kv, w_qdec, w_krope, w_qrope, w_o, router, bias,
                   gate, up, down, sgate, sup, sdown, cos, sin, out, x1_dram, x1t_dram, cw_dram):
    f32, f32r, bf16 = mybir.dt.float32, mybir.dt.float32r, mybir.dt.bfloat16
    ALU, ACT, AX = mybir.AluOpType, mybir.ActivationFunctionType, mybir.AxisListType
    ctx = ExitStack()

    def sb(name, shape, dt=f32):
        return ctx.enter_context(nc.sbuf_tensor(name, shape, dt))

    def sem(name):
        return ctx.enter_context(nc.semaphore(name))

    with ctx:
        wqkv = sb("wqkv", [P, QR + KR])
        wkvg = sb("wkvg", [QR + KR, 2 * P])
        gkv = sb("gkv", [QR + KR, 1])
        ones = sb("ones", [QR + KR, 1])
        wqd = sb("wqd", [QR, P])
        wkr = sb("wkr", [P, RD * NH])
        wqr = sb("wqr", [QR, RD * NH])
        wo = sb("wo", [P, C])
        rw = sb("rw", [P, E])
        bias_sb = sb("bias_sb", [P, E])
        cos_sb = sb("cos_sb", [P, NT, RD])
        sin_sb = sb("sin_sb", [P, NT, RD])
        ident = sb("ident", [P, P])
        identb = sb("identb", [P, P], bf16)
        maskb = sb("maskb", [P, P], bf16)
        lower = sb("lower", [P, E, E])
        mhalf = sb("mhalf", [P, NT])
        tick = sb("tick", [P, 2])
        xn = sb("xn", [P, NT, C])
        xr = sb("xr", [P, NT, C])
        xt = sb("xt", [P, T])
        qct = sb("qct", [QR + KR, T])
        sq = sb("sq", [QR + KR, T])
        ms = sb("ms", [P, NT])
        rr = sb("rr", [P, NT])
        feat = sb("feat", [P, FT, SLOTS, FD])
        turned = [sb("tk", [P, NH, RD]), sb("tq", [P, NH, RD])]
        hi = sb("hi", [P, FB, T], f32r)
        lo = sb("lo", [P, FB, T], f32r)
        ks = sb("ks", [P, NH, T], f32r)
        qs = sb("qs", [P, NH, T], f32r)
        vn = sb("vn", [P, NT, NH, HD])
        va = sb("va", [P, NT, NH * VW + SLOT - VW])
        probs = sb("probs", [P, 2, 2 * PS, T])
        nm = sb("nm", [P, 2, NT, HG])
        rows = sb("rows", [HG, 1, 2, T], f32r)
        ot = sb("ot", [P, T])
        rs = sb("rs", [P, NT, HG])
        on = sb("on", [P, NT, NH, HD])
        st6 = sb("st6", [P, NT, 6])
        mv = sb("mv", [P, NT, 2])
        ve = sb("ve", [P, NT])
        rstd = sb("rstd", [P, NT])
        x1 = sb("x1", [P, NT, C])
        x1t = sb("x1t", [P, T])
        ont = x1t
        z = xr
        sc = sb("sc", [P, NT, E])
        sbias = sb("sbias", [P, NT, E])
        t2 = sb("t2", [P, 6, NT * NG])
        gmask = sb("gmask", [P, NT, NG])
        masked = sb("masked", [P, NT, E])
        above = sb("above", [P, E, E])
        equal = sb("equal", [P, E, E])
        rank = sbias
        cw = sb("cw", [P, NT, E])
        wsum = sb("wsum", [P, 2, NT])

        wkvd = probs[:, 0, 0, :]
        psum = ctx.enter_context(nc.psum_tensor("psum", [P, 8, T], f32))

        s_w0 = sem("first_weights_loaded")
        s_w = sem("weights_loaded")
        s_wkvg = sem("kv_weights_times_g")
        s_zero = sem("pool_zeroed")
        s_const = sem("constants_made")
        CONSTS = 6
        s_ones = sem("stack_ones_made")
        s_x = sem("x_loaded")
        s_xr = sem("residual_loaded")
        s_made = [sem(f"scratch{k}_made") for k in range(2)]
        s_read = [sem(f"scratch{k}_read") for k in range(2)]
        s_qct = sem("latents_copied")
        s_ms = sem("mean_square_ready")
        s_rr = sem("inverse_rms_ready")
        s_vn = sem("next_values_copied")
        s_va = sem("values_in_place")
        s_rope = sem("rotary_added")
        s_hi = sem("high_parts_ready")
        s_stk = [[sem(f"{x}_stacked{n}") for n in range(len(SHARES))] for x in "kq"]
        s_mx = sem("max_scores_made")
        s_mxr = sem("maxima_taken")
        s_nmt = sem("maxima_transposed")
        s_mh = sem("max_hi_ready")
        s_ml = sem("max_lo_ready")
        s_row = [sem(f"max_rows_placed{g}") for g in range(GROUPS)]
        s_st = sem("scores_made")
        s_exp = sem("exponentials_ready")
        s_msk = sem("future_zeroed")
        s_pv = sem("values_weighted")
        s_oc = sem("weighted_copied")
        s_otr = sem("weighted_transposed")
        s_rs = sem("inverse_sums_ready")
        s_on = sem("heads_normalised")
        s_var = sem("variance_ready")
        s_rstd = sem("rstd_ready")
        s_x1 = sem("x1_ready")
        s_pool = sem("pool_chain")
        s_above = sem("rank_terms_ready")
        s_rank = sem("ranks_ready")
        s_compared = sem("experts_compared")
        s_cw = sem("expert_weights_ready")
        s_kept = sem("x1_stored")
        s_keptt = sem("x1t_stored")
        s_keptw = sem("expert_weights_stored")
        s_dve = {-2: sem("dve_chain_of_routing"), -1: sem("dve_chain_of_norm")}

        arena = probs[:, :, :, :].rearrange("p a s t -> p (a s t)")
        taken = [0]

        def view(size):
            taken[0] += size
            return arena[:, taken[0] - size:taken[0]]

        wdn = view(FH)
        act_out = [view(T) for _ in range(2)]
        hid = [[view(T) for _ in range(HB)] for _ in range(2)]
        picks = view(FE)[0:E, :]
        arena, taken = feat[:, :, :, :].rearrange("p a s d -> p (a s d)"), [0]
        w_in = view(3 * T).rearrange("p (n d) -> p n d", n=3)
        xd = [view(NT * C).rearrange("p (n d) -> p n d", n=NT) for _ in range(2)]
        xdt = [view(T) for _ in range(2)]
        cwd = [view(NT * E).rearrange("p (n e) -> p n e", n=NT) for _ in range(2)]
        zd = [v[:, :, :].rearrange("p h d -> p (h d)").rearrange("p (n d) -> p n d", n=NT) for v in turned]
        yd = [v[:, :, :] for v in (xn, x1)]
        w_hi, w_lo = hi[:, 0:3, :], lo[:, 0:3, :]
        x_hi, x_lo = ([v[:, 3 + q, :] for q in range(2)] for v in (hi, lo))
        cw_hi, cw_lo = ([v[0:E, 5 + q, :] for q in range(2)] for v in (hi, lo))
        picks_r = hi[0:E, 7, :]
        s_we = sem("expert_matrices_loaded")
        s_wd = sem("down_matrices_loaded")
        s_pick = sem("picks_made")
        s_wh = sem("expert_matrices_high")
        s_wl = sem("expert_matrices_low")
        s_dxt = [sem(f"chunk_x1t_loaded{q}") for q in range(2)]
        s_dx = [sem(f"chunk_x1_loaded{q}") for q in range(2)]
        s_xh = sem("chunk_high_ready")
        s_xl = sem("chunk_low_ready")
        s_ct = sem("chunk_weights_transposed")
        s_ch = sem("chunk_weights_high")
        s_cl = sem("chunk_weights_low")
        s_g = sem("gates_made")
        s_u = sem("ups_made")
        s_cb = sem("weights_spread")
        s_act = sem("gates_activated")
        s_hu = sem("hidden_multiplied")
        s_hid = sem("hidden_weighted")
        s_dn = sem("down_projected")
        s_zd = sem("residual_added")
        s_vd = sem("chunk_variance_ready")
        s_rd = sem("chunk_rstd_ready")
        s_od = sem("chunk_normalised")
        s_out = [sem(f"chunk_stored{q}") for q in range(2)]
        s_dvd = sem("dve_chain_of_experts")

        block = ctx.enter_context(nc.Block())

        @block.sync
        def _(sp):
            def load(semaphore, *pairs):
                for dst, src in pairs:
                    sp.dma_start(dst, src).then_inc(semaphore, 16)

            def store_weights(c):
                after(sp, s_cw, c + 1)
                sp.dma_start(cw_dram[c], cw[:, :, :].rearrange("p n e -> p (n e)")).then_inc(s_keptw, 16)

            def attend(b, phase):
                use = scratch_uses(b, phase)
                for item in ITEMS[phase]:
                    kind, d, u, k = item
                    c = b + d
                    if kind == "load_x":
                        after(sp, s_qct, c)
                        sp.dma_start(xn[:, :, :], x[c].rearrange("(n p) d -> p n d", p=P)).then_inc(s_x, 16)
                    elif kind == "load_residual":
                        after(sp, s_x1, NT * c)
                        sp.dma_start(xr[:, :, :], x[c].rearrange("(n p) d -> p n d", p=P)).then_inc(s_xr, 16)
                    elif kind == "stack":
                        if k == 0:
                            if u == 0:
                                n, made = use[("features", 1, NT - 1, 2)]
                                after(sp, s_read[n], made)
                            after(sp, s_exp, SB * (c - 1) + PS * SHARES[u][1])
                        n, part = k // PARTS, k % PARTS
                        stack, source = ((ks, (hi, lo, hi)), (qs, (hi, hi, lo)))[n]
                        for i in range(BH):
                            h0, h1, f0, f1 = slots_of(n, i, u)
                            sp.dma_start(stack[part * FD:part * FD + FD, h0:h1:BH, :].bitcast(f32),
                                         source[part][i * FD:i * FD + FD, f0:f1, :].bitcast(f32)).then_inc(s_stk[n][u], 16)
                    elif kind == "rows":
                        for n, ready in enumerate((s_mh, s_ml)):
                            after(sp, ready, GROUPS * c + u + 1)
                            sp.dma_start(qs[3 * FD + n:3 * FD + n + 1, HG * u:HG * u + HG, :].bitcast(f32),
                                         rows[:, 0, n, :].bitcast(f32)).then_inc(s_row[u], 16)
                    elif kind == "turn_x1":
                        after(sp, s_x1, NT * c + NT)
                        sp.dma_start(x1_dram[c].rearrange("(n p) d -> p n d", p=P), x1[:, :, :]).then_inc(s_kept, 16)
                    elif kind == "logits":
                        n, made = use[("turn_x1", -1, 0, 0)]
                        after(sp, s_read[n], made)
                        sp.dma_start(x1t_dram[c], x1t[:, :]).then_inc(s_keptt, 16)
                    elif kind == "route" and u == 6 and d == -2:
                        store_weights(c)

            load(s_w0, (wqkv[:, :], w_qkv), (wkr[:, :], w_krope), (wqr[:, :], w_qrope),
                 (cos_sb[:, :, :], cos.rearrange("(n p) d -> p n d", p=P)),
                 (sin_sb[:, :, :], sin.rearrange("(n p) d -> p n d", p=P)))
            attend(-2, "before2")
            load(s_w, (wkvd[QR:QR + KR, 0:2 * P], w_kvdec), (gkv[QR:QR + KR, :], g_kv), (wqd[:, :], w_qdec),
                 (wo[:, :], w_o), (rw[:, :], router), (bias_sb[:, :], bias.partition_broadcast(P)))
            sp.wait_ge(s_ones, 1)
            attend(-1, "before")
            attend(0, "first")
            attend(1, "second")
            attend(2, "steady")
            with sp.Fori(3, B - 2) as b:
                attend(b, "steady")
            attend(B - 2, "last2")
            attend(B - 1, "last")
            sp.wait_ge(s_hi, 3 * NT * B)
            for dst, src in ((w_in[:, 0, :], gate), (w_in[:, 1, :], up), (w_in[:, 2, 0:HS], sgate), (w_in[:, 2, HS:], sup)):
                sp.dma_start(dst, src).then_inc(s_we, 16)
            sp.wait_ge(s_kept, 16 * (B - 1))
            sp.wait_ge(s_keptt, 16 * (B - 1))
            sp.wait_ge(s_keptw, 16 * (B - 2))

            def chunk(c, q):
                if within(c, -1, B - 1):
                    after(sp, s_u, HB * c)
                    after(sp, s_ct, c)
                    sp.dma_start(xdt[1 - q], x1t_dram[c + 1]).then_inc(s_dxt[1 - q], 16)
                    sp.dma_start(cwd[1 - q].rearrange("p n e -> p (n e)"), cw_dram[c + 1]).then_inc(s_dxt[1 - q], 16)
                    after(sp, s_zd, c)
                    sp.dma_start(xd[1 - q], x1_dram[c + 1].rearrange("(n p) d -> p n d", p=P)).then_inc(s_dx[1 - q], 16)
                if within(c, 2, B + 2):
                    after(sp, s_od, NT * (c - 1))
                    sp.dma_start(out[c - 2].rearrange("(n p) d -> p n d", p=P), yd[q]).then_inc(s_out[q], 16)

            chunk(-1, 1)
            store_weights(B - 2)
            attend(B, "after")
            sp.wait_ge(s_kept, 16 * B)
            sp.wait_ge(s_keptt, 16 * B)
            sp.wait_ge(s_pv, GROUPS * B)
            for dst, src, n in ((wdn[:, 0:FE], down, ROUTED), (wdn[:, FE:], sdown, HB - ROUTED)):
                sp.dma_start(dst.rearrange("p (k c) -> p k c", c=C), src.rearrange("(k p) c -> p k c", p=P)).then_inc(s_wd, 16)
            chunk(0, 0)
            chunk(1, 1)
            attend(B + 1, "after2")
            sp.wait_ge(s_keptw, 16 * B)
            chunk(2, 0)
            chunk(3, 1)
            with sp.Fori(2, B // 2 - 1) as i:
                chunk(2 * i, 0)
                chunk(2 * i + 1, 1)
            chunk(B - 2, 0)
            chunk(B - 1, 1)
            chunk(B, 0)
            chunk(B + 1, 1)
            for q in range(2):
                sp.wait_ge(s_out[q], 16 * (B // 2))

        @block.gpsimd
        def _(pool):
            pool.memset(ident[:, :], 0.0).then_inc(s_zero, 1)
            pool.memset(identb[:, :], 0.0).then_inc(s_zero, 1)
            pool.memset(maskb[:, :], 0.0).then_inc(s_zero, 1)
            pool.memset(lower[:, :, :], 0.0).then_inc(s_zero, 1)
            pool.memset(feat[:, :, 2 * NH:, :], 0.0).then_inc(s_zero, 1)
            pool.memset(ones[:, :], 1.0).then_inc(s_const, 1)
            pool.memset(mhalf[:, :], -0.5).then_inc(s_const, 1)
            pool.wait_ge(s_zero, 5)
            for m in (ident, identb):
                pool.affine_select(out=m[:, :], in_=m[:, :], compare_op=ALU.not_equal, fill=1.0, base=0,
                                   pattern=[[-1, P]], channel_multiplier=1).then_inc(s_const, 1)
            pool.affine_select(out=maskb[:, :], in_=maskb[:, :], compare_op=ALU.is_ge, fill=HIDDEN, base=0,
                               pattern=[[-1, P]], channel_multiplier=1).then_inc(s_const, 1)
            pool.affine_select(out=lower[:, :, :], in_=lower[:, :, :], compare_op=ALU.is_ge, fill=1.0, base=0,
                               pattern=[[-1, E], [1, E]], channel_multiplier=0).then_inc(s_zero, 1)
            pool.wait_ge(s_zero, 6)
            pool.memset(ks[96:P, :, :].bitcast(f32), 1.0).then_inc(s_ones, 1)
            pool.wait_ge(s_ones, 1)

            def attend(b, phase, chosen=slice(None)):
                use = scratch_uses(b, phase)
                for item in ITEMS[phase][chosen]:
                    kind, d, u, k = item
                    c = b + d
                    if kind == "contents":
                        if u == 0:
                            after(pool, s_va, c)
                        after(pool, s_ms, NT * c + u + 1)
                        pool.tensor_tensor(out=rr[:, u:u + 1], in0=ms[:, u:u + 1], in1=mhalf[:, 0:1],
                                           op=ALU.pow).then_inc(s_rr, 1)
                    elif kind in ("k_rope", "q_rope"):
                        n = kind == "q_rope"
                        bank, made = use[item]
                        after(pool, s_read[bank], made)
                        rope = feat[:, u % FT, NH * n:NH * n + NH, HD:]
                        pool.tensor_tensor(out=rope, in0=rope, in1=turned[n][:, :, :], op=ALU.add).then_inc(s_rope, 1)
                    elif kind == "values":
                        after(pool, s_pv, GROUPS * c)
                        after(pool, s_vn, NT * c + NT)
                        pool.tensor_tensor(out=va[:, :, 0:NH * VW].rearrange("p n (h d) -> p n h d", h=NH)[:, :, :, 0:HD],
                                           in0=vn[:, :, :, :], in1=rr[:, :].unsqueeze(2).unsqueeze(3).to_broadcast([P, NT, NH, HD]),
                                           op=ALU.mult).then_inc(s_va, 1)
                    elif kind == "exp" and k == PS - 1:
                        after(pool, s_msk, 3 * (PAIRS * c + u))
                        after(pool, s_exp, PS * (PAIRS * c + u) + PS)
                        pool.tensor_tensor(out=tick[:, 1:2], in0=mhalf[:, 0:1], in1=mhalf[:, 0:1], op=ALU.add)
                        at = probs[:, (u // 2) % 2, :, :]
                        s = PS * (u % 2)
                        for part in (at[:, s:s + 4, 0:P], at[:, s + 1:s + 4:2, 3 * P:4 * P],
                                     at[:, s + 4, :].rearrange("p (a c) -> p a c", a=2)[:, :, 0:P]):
                            pool.affine_select(out=part, in_=part, compare_op=ALU.is_ge, fill=0.0, base=0,
                                               pattern=[[0, part.shape[1]], [1, P]],
                                               channel_multiplier=-1).then_inc(s_msk, 1)
                    elif kind == "route" and 2 <= u < 6:
                        n = NT * c + u - 2
                        after(pool, s_compared, n + 1)
                        pool.tensor_tensor(out=equal[:, :, :], in0=equal[:, :, :], in1=lower[:, :, :],
                                           op=ALU.mult).then_inc(s_pool, 1)
                        after(pool, s_pool, n + 1)
                        pool.tensor_tensor(out=above[:, :, :], in0=above[:, :, :], in1=equal[:, :, :],
                                           op=ALU.add).then_inc(s_above, 1)
                    elif kind == "x1":
                        after(pool, s_var, c + 1)
                        pool.tensor_tensor(out=rstd[:, :], in0=ve[:, :], in1=mhalf[:, :], op=ALU.pow).then_inc(s_rstd, 1)

            attend(-2, "before2")
            attend(-1, "before")
            attend(0, "first")
            attend(1, "second")
            attend(2, "steady")
            with pool.Fori(3, B - 2) as b:
                attend(b, "steady")
            attend(B - 2, "last2")
            attend(B - 1, "last")
            attend(B, "after")

            pool.wait_ge(s_pv, GROUPS * B)
            pool.memset(picks, 1.0).then_inc(s_pick, 1)
            pool.wait_ge(s_pick, 1)
            pool.affine_select(out=picks, in_=picks, compare_op=ALU.is_ge, fill=0.0, base=0,
                               pattern=[[1, FE]], channel_multiplier=-HE).then_inc(s_pick, 1)
            pool.wait_ge(s_pick, 2)
            pool.affine_select(out=picks, in_=picks, compare_op=ALU.is_ge, fill=0.0, base=HE - 1,
                               pattern=[[-1, FE]], channel_multiplier=HE).then_inc(s_pick, 1)

            def chunk(c, q):
                for kind, n, _ in CHUNK_ITEMS:
                    if kind == "hidden" and last_routing(c, n):
                        attend(B + 1, "after2", last_routing(c, n))
                    elif kind == "norm" and within(c, 1, B + 1):
                        after(pool, s_vd, c)
                        pool.tensor_tensor(out=rstd[:, :], in0=ve[:, :], in1=mhalf[:, :], op=ALU.pow).then_inc(s_rd, 1)

            chunk(0, 0)
            chunk(1, 1)
            chunk(2, 0)
            chunk(3, 1)
            with pool.Fori(2, B // 2 - 1) as i:
                chunk(2 * i, 0)
                chunk(2 * i + 1, 1)
            chunk(B - 2, 0)
            chunk(B - 1, 1)
            chunk(B, 0)
            chunk(B + 1, 1)

        @block.scalar
        def _(act):
            act.wait_ge(s_const, CONSTS)

            def attend(b, phase):
                use = scratch_uses(b, phase)
                for item in ITEMS[phase]:
                    kind, d, u, k = item
                    c = b + d
                    if item in use:
                        n, made = use[item]
                        bank = psum[:, SCRATCH_BANKS[n], :]
                    if kind == "turn_x":
                        after(act, s_made[n], made)
                        act.activation(xt[:, :], bank, ACT.Copy).then_inc(s_read[n], 1)
                    elif kind == "latents":
                        after(act, s_made[n], made)
                        act.activation(qct[:, :], bank[0:QR + KR, :], ACT.Copy).then_inc(s_qct, 1)
                        act.activation(sq[:, :], bank[0:QR + KR, :], ACT.Square).then_inc(s_read[n], 1)
                    elif kind == "contents":
                        after(act, s_va, c)
                        after(act, s_rr, NT * c + u + 1)
                        parts = bank[:, 0:3 * P].rearrange("p (n h d) -> p n h d", n=3, h=NH)
                        act.activation(vn[:, u, :, :], parts[:, 2, :, :], ACT.Copy).then_inc(s_vn, 1)
                        act.activation(feat[:, u % FT, NH:2 * NH, 0:HD], parts[:, 0, :, :], ACT.Copy)
                        act.activation(feat[:, u % FT, 0:NH, 0:HD], parts[:, 1, :, :], ACT.Copy,
                                       scale=rr[:, u:u + 1]).then_inc(s_read[n], 1)
                    elif kind == "features":
                        if u == 0:
                            for which in range(2):
                                for share in range(len(SHARES)):
                                    blocks = {f for i in range(BH) for f in range(*slots_of(which, i, share)[2:])}
                                    if blocks & set(range(4 * k, 4 * k + 4)):
                                        after(act, s_stk[which][share], STACKED * c)
                        after(act, s_made[n], made)
                        f0, f1 = 4 * k, min(4 * k + 4, FB)
                        act.activation(hi[0:FR, f0:f1, u * P:u * P + P],
                                       bank[0:FR, 0:(f1 - f0) * P].rearrange("p (f t) -> p f t", t=P),
                                       ACT.Copy).then_inc(s_hi, 1)
                    elif kind == "exp":
                        m = PS * u + k
                        if m % (2 * PS) == 0:
                            after(act, s_pv, GROUPS * c + u // 2 - 1)
                        after(act, s_st, SB * c + m + 1)
                        act.activation(probs[:, (u // 2) % 2, PS * (u % 2) + k, :], psum[:, 4 + m % 2, :], ACT.Exp,
                                       scale=SCALE).then_inc(s_exp, 1)
                    elif kind == "rows":
                        after(act, s_row[(u - 1) % GROUPS], 32 * c + 32 if u else 32 * c)
                        after(act, s_nmt, GROUPS * c + u + 1)
                        act.activation(rows[:, 0, 0, :], psum[0:HG, 7, :], ACT.Copy).then_inc(s_mh, 1)
                    elif kind == "pv":
                        after(act, s_otr, GROUPS * c + u)
                        after(act, s_pv, GROUPS * c + u + 1)
                        act.activation(ot[:, :], psum[:, 7, :], ACT.Copy).then_inc(s_oc, 1)
                    elif kind == "turn_heads":
                        after(act, s_keptt, 16 * c)
                        after(act, s_made[n], made)
                        act.activation(ont[:, :], bank, ACT.Copy).then_inc(s_read[n], 1)
                    elif kind == "turn_x1":
                        after(act, s_made[n], made)
                        act.activation(x1t[:, :], bank, ACT.Copy).then_inc(s_read[n], 1)
                    elif kind == "logits":
                        after(act, s_cw, c)
                        after(act, s_made[n], made)
                        act.activation(sc[:, :, :], bank[:, 0:NT * E].rearrange("p (n e) -> p n e", n=NT), ACT.Exp,
                                       scale=-1.0).then_inc(s_read[n], 1)

            attend(-2, "before2")
            attend(-1, "before")
            attend(0, "first")
            attend(1, "second")
            attend(2, "steady")
            with act.Fori(3, B - 2) as b:
                attend(b, "steady")
            attend(B - 2, "last2")
            attend(B - 1, "last")
            for stacked in s_stk[0] + s_stk[1]:
                act.wait_ge(stacked, STACKED * B)
            act.wait_ge(s_we, 16 * 4)
            act.activation(w_hi, w_in, ACT.Copy).then_inc(s_wh, 1)

            def chunk(c, q):
                for kind, n, block in CHUNK_ITEMS:
                    if kind == "split" and within(c, -1, B - 1):
                        after(act, s_dxt[1 - q], 32 * count_of(c + 1))
                        after(act, s_u, HB * c)
                        act.activation(x_hi[1 - q], xdt[1 - q], ACT.Copy).then_inc(s_xh, 1)
                    elif kind == "weights" and within(c, -1, B - 1):
                        after(act, s_ct, c + 2)
                        act.activation(cw_hi[1 - q], psum[0:E, 4, :], ACT.Copy).then_inc(s_ch, 1)
                    elif kind == "hidden" and within(c, 0, B):
                        after(act, s_hu, HB * c + n - 1)
                        after(act, s_g, HB * c + n + 1)
                        act.activation(act_out[n % 2], psum[:, n % 2, :], ACT.Silu).then_inc(s_act, 1)

            chunk(-1, 1)
            attend(B, "after")

            act.wait_ge(s_pick, 3)
            act.activation(picks_r, picks, ACT.Copy).then_inc(s_wh, 1)
            chunk(0, 0)
            chunk(1, 1)
            chunk(2, 0)
            chunk(3, 1)
            with act.Fori(2, B // 2 - 1) as i:
                chunk(2 * i, 0)
                chunk(2 * i + 1, 1)
            chunk(B - 2, 0)
            chunk(B - 1, 1)
            chunk(B, 0)
            chunk(B + 1, 1)

        @block.vector
        def _(dve):
            dve.memset(va[:, :, :], 1.0).then_inc(s_const, 1)
            dve.wait_ge(s_w0, 16 * 5)
            LINKS = {-2: 19, -1: 2}

            linked = {}

            def attend(b, phase, chosen=slice(None)):
                use = scratch_uses(b, phase)
                if chosen.start in (None, 0):
                    linked.update({-2: 0, -1: 0})

                def link(ins, chain, c):
                    linked[chain] += 1
                    ins.then_inc(s_dve[chain], 1)
                    after(dve, s_dve[chain], LINKS[chain] * c + linked[chain])

                for item in ITEMS[phase][chosen]:
                    kind, d, u, k = item
                    c = b + d
                    if item in use:
                        n, made = use[item]
                        bank = psum[:, SCRATCH_BANKS[n], :]
                    if kind in ("k_rope", "q_rope"):
                        which = kind == "q_rope"
                        after(dve, s_rope, 2 * (NT * c + u - 1) + which + 1)
                        after(dve, s_made[n], made)
                        src = bank.rearrange("p (h d) -> p h d", h=NH)
                        H = RD // 2
                        dve.tensor_tensor(feat[:, u % FT, NH * which:NH * which + NH, HD:], src,
                                          cos_sb[:, u, :].unsqueeze(1).to_broadcast([P, NH, RD]), ALU.mult)
                        for a_, c_ in ((0, H), (H, 0)):
                            a = dve.tensor_tensor(turned[which][:, :, a_:a_ + H], src[:, :, c_:c_ + H],
                                                  sin_sb[:, u, a_:a_ + H].unsqueeze(1).to_broadcast([P, NH, H]), ALU.mult)
                        a.then_inc(s_read[n], 1)
                    elif kind == "contents":
                        after(dve, s_made[n], made)
                        dve.tensor_scalar(ms[:, u:u + 1], bank[:, 3 * P:3 * P + 1], 1.0 / KR, RMS_EPS,
                                          ALU.mult, ALU.add).then_inc(s_ms, 1)
                    elif kind == "features":
                        after(dve, s_hi, 3 * (NT * c + u) + k + 1)
                        f0, f1 = 4 * k, min(4 * k + 4, FB)
                        dve.tensor_tensor(lo[0:FR, f0:f1, u * P:u * P + P],
                                          bank[0:FR, 0:(f1 - f0) * P].rearrange("p (f t) -> p f t", t=P),
                                          hi[0:FR, f0:f1, u * P:u * P + P].bitcast(f32), ALU.subtract).then_inc(s_read[n], 1)
                    elif kind == "max":
                        m = PS * u + k
                        g = u // 2
                        if m % (2 * PS) == 0:
                            after(dve, s_nmt, GROUPS * c + g - 1)
                        after(dve, s_mx, SB * c + m + 1)
                        if k == PS - 1:
                            a = dve.tensor_reduce(nm[:, g % 2, 1, 2 * (u % 2):2 * (u % 2) + 2],
                                                  psum[:, MAX_BANKS[m % 3], :].rearrange("p (a c) -> p a c", a=2), AX.X, ALU.max, negate=True)
                        else:
                            for i, qt, c0 in MAX_STEPS[k]:
                                h = 2 * (u % 2) + i
                                a = dve.tensor_reduce(nm[:, g % 2, qt, h:h + 1], psum[:, MAX_BANKS[m % 3], c0:c0 + (qt + 1) * P],
                                                      AX.X, ALU.max, negate=True)
                        a.then_inc(s_mxr, 1)
                    elif kind == "rows":
                        after(dve, s_mh, GROUPS * c + u + 1)
                        dve.tensor_tensor(rows[:, 0, 1, :], psum[0:HG, 7, :], rows[:, 0, 0, :].bitcast(f32),
                                          ALU.subtract).then_inc(s_ml, 1)
                    elif kind == "turn":
                        after(dve, s_otr, GROUPS * c + u + 1)
                        heads = psum[:, 7, :].rearrange("p (n h c) -> p n h c", n=NT, h=HG)
                        dve.reciprocal(rs[:, :, :].unsqueeze(3), heads[:, :, :, HD:HD + 1]).then_inc(s_rs, 1)
                        after(dve, s_rs, GROUPS * c + u + 1)
                        dve.tensor_tensor(on[:, :, HG * u:HG * u + HG, :], heads[:, :, :, 0:HD],
                                          rs[:, :, :].unsqueeze(3).to_broadcast([P, NT, HG, HD]),
                                          ALU.mult).then_inc(s_on, 1)
                    elif kind == "project_out":
                        after(dve, s_xr, 16 * c + 16)
                        after(dve, s_made[n], made)
                        dve.tensor_tensor(z[:, :, :], bank.rearrange("p (n d) -> p n d", n=NT), xr[:, :, :],
                                          ALU.add).then_inc(s_read[n], 1)
                        after(dve, s_read[n], made)
                        for t in range(NT):
                            a = dve.bn_stats(st6[:, t, :], z[:, t, :])
                        link(a, -1, c)
                        dve.tensor_copy(tick[:, 0:1], mhalf[:, 0:1])
                        for t in range(NT):
                            a = dve.bn_aggr(mv[:, t, :], st6[:, t, :])
                        link(a, -1, c)
                        dve.tensor_scalar(ve[:, :].unsqueeze(2), mv[:, :, 1:2], LN_EPS, None, ALU.add).then_inc(s_var, 1)
                    elif kind == "x1":
                        after(dve, s_rstd, c + 1)
                        after(dve, s_kept, 16 * c)
                        for t in range(NT):
                            dve.tensor_scalar(x1[:, t, :], z[:, t, :], mv[:, t, 0:1], rstd[:, t:t + 1], ALU.subtract,
                                              ALU.mult).then_inc(s_x1, 1)
                    elif kind == "route" and u == 0:
                        linked[-2] = 0
                        logits = use.get(("logits", d, 0, 0)) if d == -1 else None
                        for n in range(2):
                            after(dve, s_read[n], logits[1] if logits and n == logits[0] else use["start"])
                        link(dve.tensor_scalar(sc[:, :, :], sc[:, :, :], 1.0, None, ALU.add), -2, c)
                        link(dve.reciprocal(sc[:, :, :], sc[:, :, :]), -2, c)
                        link(dve.tensor_tensor(sbias[:, :, :], sc[:, :, :],
                                               bias_sb[:, :].unsqueeze(1).to_broadcast([P, NT, E]), ALU.add), -2, c)
                        four = sbias[:, :, :].rearrange("p n (g e) -> p (n g) e", g=NG)
                        a0, a1, a2, a3 = (four[:, :, i:i + 1] for i in range(EG))
                        s0, s1, s2, s3, s4, s5 = (t2[:, i, :].unsqueeze(2) for i in range(6))
                        dve.tensor_tensor(s0, a0, a1, ALU.max)
                        dve.tensor_tensor(s1, a0, a1, ALU.min)
                        dve.tensor_tensor(s2, a2, a3, ALU.max)
                        link(dve.tensor_tensor(s3, a2, a3, ALU.min), -2, c)
                        dve.tensor_tensor(s4, s0, s2, ALU.min)
                        link(dve.tensor_tensor(s5, s1, s3, ALU.max), -2, c)
                        link(dve.tensor_tensor(s1, s0, s2, ALU.max), -2, c)
                        link(dve.tensor_tensor(s3, s4, s5, ALU.max), -2, c)
                        link(dve.tensor_tensor(s0, s1, s3, ALU.add), -2, c)
                    elif kind == "route" and u == 1:
                        gs = t2[:, 0, :].rearrange("p (n g) -> p n g", n=NT)
                        NG2 = [P, NT, NG, NG]
                        gt, eq = (v[:, 0:NG, :].rearrange("p n (g f) -> p n g f", g=NG) for v in (above, equal))
                        mine, other = gs.unsqueeze(3).to_broadcast(NG2), gs.unsqueeze(2).to_broadcast(NG2)
                        after(dve, s_rank, NT * c)
                        dve.tensor_tensor(gt, other, mine, ALU.is_gt)
                        link(dve.tensor_tensor(eq, other, mine, ALU.is_equal), -2, c)
                        link(dve.tensor_tensor(eq, eq, lower[:, 0:NG, 0:NG].unsqueeze(1).to_broadcast(NG2), ALU.mult), -2, c)
                        link(dve.tensor_tensor(gt, gt, eq, ALU.add), -2, c)
                        link(dve.tensor_reduce(gmask[:, :, :], gt, AX.X, ALU.add), -2, c)
                        link(dve.tensor_scalar(gmask[:, :, :], gmask[:, :, :], TOPG - 0.5, -3e38, ALU.is_gt, ALU.mult), -2, c)
                        link(dve.tensor_tensor(masked[:, :, :].rearrange("p n (g e) -> p (n g) e", g=NG),
                                               sbias[:, :, :].rearrange("p n (g e) -> p (n g) e", g=NG),
                                               gmask[:, :, :].rearrange("p n g -> p (n g)").unsqueeze(2).to_broadcast([P, NT * NG, EG]),
                                               ALU.add), -2, c)
                    elif kind == "route":
                        if u >= 3:
                            n = NT * c + u - 3
                            after(dve, s_above, n + 1)
                            dve.tensor_reduce(rank[:, u - 3, :], above[:, :, :], AX.X, ALU.add).then_inc(s_rank, 1)
                        if u < 6:
                            n = NT * c + u - 2
                            v = masked[:, u - 2, :]
                            mine, other = v.unsqueeze(2).to_broadcast([P, E, E]), v.unsqueeze(1).to_broadcast([P, E, E])
                            after(dve, s_rank, n)
                            dve.tensor_tensor(above[:, :, :], other, mine, ALU.is_gt)
                            dve.tensor_tensor(equal[:, :, :], other, mine, ALU.is_equal).then_inc(s_compared, 1)
                    if kind == "route" and u == 6:
                        after(dve, s_rank, NT * c + NT)
                        link(dve.tensor_scalar(rank[:, :, :], rank[:, :, :], TOPK - 0.5, None, ALU.is_lt), -2, c)
                        link(dve.tensor_tensor(rank[:, :, :], rank[:, :, :], sc[:, :, :], ALU.mult), -2, c)
                        link(dve.tensor_reduce(wsum[:, 0, :], rank[:, :, :], AX.X, ALU.add), -2, c)
                        link(dve.tensor_scalar(wsum[:, 0, :], wsum[:, 0, :], 1e-20, None, ALU.add), -2, c)
                        link(dve.reciprocal(wsum[:, 1, :], wsum[:, 0, :]), -2, c)
                        after(dve, s_keptw, 16 * c)
                        dve.tensor_tensor(cw[:, :, :], rank[:, :, :], wsum[:, 1, :].unsqueeze(2).to_broadcast([P, NT, E]),
                                          ALU.mult).then_inc(s_cw, 1)
                assert chosen.start is not None or all(linked[d] in (0, LINKS[d]) for d in linked)

            attend(-2, "before2")
            dve.wait_ge(s_w, 16 * 6)
            dve.tensor_scalar(wkvg[QR:QR + KR, :], wkvd[QR:QR + KR, 0:2 * P], gkv[QR:QR + KR, 0:1], None,
                              ALU.mult).then_inc(s_wkvg, 1)
            attend(-1, "before")
            attend(0, "first")
            attend(1, "second")
            attend(2, "steady")
            with dve.Fori(3, B - 2) as b:
                attend(b, "steady")
            attend(B - 2, "last2")
            attend(B - 1, "last")
            dve.wait_ge(s_wh, 1)
            dve.tensor_tensor(w_lo, w_in, w_hi.bitcast(f32), ALU.subtract).then_inc(s_wl, 1)
            DLINKS = 2

            def chunk(c, q):
                def link(ins, n):
                    ins.then_inc(s_dvd, 1)
                    after(dve, s_dvd, DLINKS * (c - 1) + n)

                for kind, n, block in CHUNK_ITEMS:
                    if kind == "split" and within(c, -1, B - 1):
                        after(dve, s_xh, c + 2)
                        dve.tensor_tensor(x_lo[1 - q], xdt[1 - q], x_hi[1 - q].bitcast(f32), ALU.subtract).then_inc(s_xl, 1)
                    elif kind == "weights" and within(c, -1, B - 1):
                        after(dve, s_ch, c + 2)
                        dve.tensor_tensor(cw_lo[1 - q], psum[0:E, 4, :], cw_hi[1 - q].bitcast(f32),
                                          ALU.subtract).then_inc(s_cl, 1)
                    elif kind == "hidden" and within(c, 0, B):
                        after(dve, s_act, HB * c + n + 1)
                        after(dve, s_u, HB * c + n + 1)
                        h = hid[q][block]
                        dve.tensor_tensor(h, psum[:, 2 + n % 2, :], act_out[n % 2], ALU.mult).then_inc(s_hu, 1)
                        if block < ROUTED:
                            after(dve, s_hu, HB * c + n + 1)
                            after(dve, s_cb, ROUTED * c + block + 1)
                            dve.tensor_tensor(h, psum[:, 4 + block % 2, :], h, ALU.mult).then_inc(s_hid, 1)
                        if last_routing(c, n):
                            attend(B + 1, "after2", last_routing(c, n))
                    elif kind == "norm" and within(c, 1, B + 1):
                        after(dve, s_dx[1 - q], 16 * count_of(c - 1))
                        after(dve, s_dn, NT * c)
                        dve.tensor_tensor(zd[1 - q], psum[:, 6 + 1 - q, :].rearrange("p (n d) -> p n d", n=NT), xd[1 - q],
                                          ALU.add).then_inc(s_zd, 1)
                        after(dve, s_zd, c)
                        for t in range(NT):
                            a = dve.bn_stats(st6[:, t, :], zd[1 - q][:, t, :])
                        link(a, 1)
                        dve.tensor_copy(tick[:, 0:1], mhalf[:, 0:1])
                        for t in range(NT):
                            a = dve.bn_aggr(mv[:, t, :], st6[:, t, :])
                        link(a, 2)
                        dve.tensor_scalar(ve[:, :].unsqueeze(2), mv[:, :, 1:2], LN_EPS, None, ALU.add).then_inc(s_vd, 1)
                    elif kind == "out" and within(c, 2, B + 2):
                        after(dve, s_out[q], 16 * (count_of(c - 2) - 1))
                        after(dve, s_rd, c - 1)
                        for t in range(NT):
                            dve.tensor_scalar(yd[q][:, t, :], zd[q][:, t, :], mv[:, t, 0:1], rstd[:, t:t + 1],
                                              ALU.subtract, ALU.mult).then_inc(s_od, 1)

            chunk(-1, 1)
            attend(B, "after")

            chunk(0, 0)
            chunk(1, 1)
            chunk(2, 0)
            chunk(3, 1)
            with dve.Fori(2, B // 2 - 1) as i:
                chunk(2 * i, 0)
                chunk(2 * i + 1, 1)
            chunk(B - 2, 0)
            chunk(B - 1, 1)
            chunk(B, 0)
            chunk(B + 1, 1)

        @block.tensor
        def _(pe):
            pe.wait_ge(s_w0, 16 * 5)
            pe.wait_ge(s_const, CONSTS)

            def attend(b, phase):
                use = scratch_uses(b, phase)

                def wait_use(item):
                    after(pe, s_read[use[item][0]], use[item][1])

                for item in ITEMS[phase]:
                    kind, d, u, k = item
                    c = b + d
                    at = slice(u * P, u * P + P)
                    if item in use:
                        n, made = use[item]
                        bank = psum[:, SCRATCH_BANKS[n], :]
                        after(pe, s_read[n], made - 1)
                    if kind == "turn_x":
                        after(pe, s_x, 16 * c + 16)
                        for t in range(NT):
                            a = pe.transpose(bank[:, t * P:t * P + P], xn[:, t, :], ident[:, :])
                        a.then_inc(s_made[n], 1)
                    elif kind == "latents":
                        wait_use(("turn_x", d, 0, 0))
                        pe.matmul(bank[0:QR + KR, :], wqkv[:, :], xt[:, :], start=True, stop=True).then_inc(s_made[n], 1)
                    elif kind == "k_rope":
                        pe.matmul(bank, xt[:, at], wkr[:, :], start=True, stop=True).then_inc(s_made[n], 1)
                    elif kind == "q_rope":
                        if u == 0:
                            wait_use(("latents", 2, 0, 0))
                        pe.matmul(bank, qct[0:QR, at], wqr[:, :], start=True, stop=True).then_inc(s_made[n], 1)
                    elif kind == "contents":
                        pe.matmul(bank[:, 0:P], qct[0:QR, at], wqd[:, :], start=True, stop=True)
                        pe.matmul(bank[:, P:3 * P], qct[QR:QR + KR, at], wkvg[QR:QR + KR, :], start=True, stop=True)
                        pe.matmul(bank[:, 3 * P:3 * P + 1], sq[QR:QR + KR, at], ones[QR:QR + KR, :],
                                  start=True, stop=True).then_inc(s_made[n], 1)
                    elif kind == "features":
                        if k == 0:
                            after(pe, s_rope, 2 * (NT * c + u) + 2)
                            wait_use(("contents", d, u, 0))
                        tile = feat[:, u % FT, :, :].rearrange("p s d -> p (s d)")
                        for f in range(4 * k, min(4 * k + 4, FB)):
                            a = pe.transpose(bank[0:FR, (f - 4 * k) * P:(f - 4 * k) * P + P],
                                             tile[:, f * FR:f * FR + FR], ident[:, :])
                        a.then_inc(s_made[n], 1)
                    elif kind == "max":
                        m = PS * u + k
                        if (u in (u0 for u0, _ in SHARES)) and k == 0:
                            share = [u0 for u0, _ in SHARES].index(u)
                            for stacked in s_stk:
                                after(pe, stacked[share], STACKED * c + STACKED)
                        after(pe, s_mxr, SB * c + (m - 2 if m >= 3 else MAX_FREE[m]))
                        for i, qt, c0 in MAX_STEPS[k]:
                            w = (qt + 1) * P
                            dst = psum[:, MAX_BANKS[m % 3], c0:c0 + w]
                            pe.matmul(dst, qs[0:3 * FD, 2 * u + i, qt * P:qt * P + P],
                                      ks[0:3 * FD, 2 * u + i, 0:w], start=True, stop=False)
                            a = pe.matmul(dst[:, w - P:w], identb[:, :], maskb[:, :], start=False, stop=True)
                        a.then_inc(s_mx, 1)
                    elif kind == "rows":
                        after(pe, s_mxr, SB * c + 2 * PS * (u + 1))
                        after(pe, s_ml, GROUPS * c + u)
                        after(pe, s_on, GROUPS * c + u - 1)
                        for qt in range(NT):
                            a = pe.transpose(psum[0:HG, 7, qt * P:qt * P + P], nm[:, u % 2, qt, :], ident[:, :])
                        a.then_inc(s_nmt, 1)
                    elif kind == "exp":
                        m = PS * u + k
                        if m % (2 * PS) == 0:
                            after(pe, s_row[u // 2], 32 * c + 32)
                        after(pe, s_exp, SB * c + m - 1)
                        for i, kt, c0 in EXP_STEPS[k]:
                            h = 2 * u + i
                            w = T - kt * P
                            a = pe.matmul(psum[:, 4 + m % 2, c0:c0 + w], ks[0:3 * FD + 2, h, kt * P:kt * P + P],
                                          qs[0:3 * FD + 2, h, kt * P:T], start=True, stop=True)
                        a.then_inc(s_st, 1)
                    elif kind == "pv":
                        if u == 0:
                            after(pe, s_va, c + 1)
                        after(pe, s_msk, 6 * (GROUPS * c + u) + 6)
                        after(pe, s_ml, GROUPS * c + u + 2 if phase != "after" else GROUPS * B)
                        after(pe, s_on, GROUPS * c + u)
                        for kt in range(NT):
                            for j in range(HG):
                                i, s = j % 2, PS * (j // 2)
                                slot, c0 = ((s + 4, 2 * P * i) if kt == 2 else
                                            (s + 2 * i + (kt > 0), 3 * P if kt == 3 else 0))
                                w = T - kt * P
                                h = HG * u + j
                                a = pe.matmul(psum[SLOT * j:SLOT * j + SLOT, 7, kt * P:T], va[:, kt, h * VW:h * VW + SLOT],
                                              probs[:, u % 2, slot, c0:c0 + w], start=kt == 0, stop=kt == NT - 1)
                        a.then_inc(s_pv, 1)
                    elif kind == "turn":
                        after(pe, s_oc, GROUPS * c + u + 1)
                        for qt in range(NT):
                            a = pe.transpose(psum[:, 7, qt * P:qt * P + P], ot[:, qt * P:qt * P + P], ident[:, :])
                        a.then_inc(s_otr, 1)
                    elif kind == "turn_heads":
                        after(pe, s_on, GROUPS * c + GROUPS)
                        for t in range(NT):
                            a = pe.transpose(bank[:, t * P:t * P + P], on[:, t, :, :].rearrange("p h d -> p (h d)"), ident[:, :])
                        a.then_inc(s_made[n], 1)
                    elif kind == "project_out":
                        wait_use(("turn_heads", d, 0, 0))
                        for t in range(NT):
                            a = pe.matmul(bank[:, t * P:t * P + P], ont[:, t * P:t * P + P], wo[:, :], start=True, stop=True)
                        a.then_inc(s_made[n], 1)
                    elif kind == "turn_x1":
                        after(pe, s_x1, NT * c + NT)
                        for t in range(NT):
                            a = pe.transpose(bank[:, t * P:t * P + P], x1[:, t, :], ident[:, :])
                        a.then_inc(s_made[n], 1)
                    elif kind == "logits":
                        wait_use(("turn_x1", d, 0, 0))
                        for t in range(NT):
                            a = pe.matmul(bank[:, t * E:t * E + E], x1t[:, t * P:t * P + P], rw[:, :], start=True, stop=True)
                        a.then_inc(s_made[n], 1)

            attend(-2, "before2")
            pe.wait_ge(s_w, 16 * 6)
            pe.wait_ge(s_wkvg, 1)
            attend(-1, "before")
            attend(0, "first")
            attend(1, "second")
            attend(2, "steady")
            with pe.Fori(3, B - 2) as b:
                attend(b, "steady")
            attend(B - 2, "last2")
            attend(B - 1, "last")
            pe.wait_ge(s_mxr, SB * B)
            pe.wait_ge(s_exp, SB * B)

            def split_product(dst, cols, q):
                which, at = cols // T, slice(cols % T, cols % T + P)
                pe.matmul(dst, w_hi[:, which, at], x_hi[q], start=True, stop=False)
                pe.matmul(dst, w_hi[:, which, at], x_lo[q], start=False, stop=False)
                return pe.matmul(dst, w_lo[:, which, at], x_hi[q], start=False, stop=True)

            def chunk(c, q):
                for kind, n, block in CHUNK_ITEMS:
                    if kind == "weights" and within(c, -1, B - 1):
                        after(pe, s_dxt[1 - q], 32 * count_of(c + 1))
                        after(pe, s_hid, ROUTED * c + ROUTED - 1)
                        for t in range(NT):
                            a = pe.transpose(psum[0:E, 4, t * P:t * P + P], cwd[1 - q][:, t, :], ident[:, :])
                        a.then_inc(s_ct, 1)
                    elif kind == "hidden" and within(c, 0, B):
                        if n == 0:
                            after(pe, s_xl, c + 1)
                        at = block * P if block < ROUTED else 2 * T + (block - ROUTED) * P
                        step = T if block < ROUTED else HS
                        after(pe, s_act, HB * c + n - 1)
                        split_product(psum[:, n % 2, :], at, q).then_inc(s_g, 1)
                        after(pe, s_hu, HB * c + n - 1)
                        split_product(psum[:, 2 + n % 2, :], at + step, q).then_inc(s_u, 1)
                        if block < ROUTED:
                            if block == 0:
                                after(pe, s_cl, c + 1)
                            after(pe, s_hid, ROUTED * c + block - 1)
                            cols = slice(block * P, block * P + P)
                            dst = psum[:, 4 + block % 2, :]
                            pe.matmul(dst, picks_r[:, cols], cw_hi[q], start=True, stop=False)
                            pe.matmul(dst, picks_r[:, cols], cw_lo[q], start=False, stop=True).then_inc(s_cb, 1)
                    elif kind == "down" and within(c, 1, B + 1):
                        if n == 0:
                            after(pe, s_wd, 32)
                            after(pe, s_hu, HB * c)
                            after(pe, s_hid, ROUTED * c)
                            after(pe, s_zd, c - 2)
                        for k in range(HB):
                            a = pe.matmul(psum[:, 6 + 1 - q, n * P:n * P + P], hid[1 - q][k][:, n * P:n * P + P],
                                          wdn[:, k * C:k * C + C], start=k == 0, stop=k == HB - 1)
                        a.then_inc(s_dn, 1)

            chunk(-1, 1)
            attend(B, "after")

            pe.wait_ge(s_on, GROUPS * B)
            for n in range(2):
                pe.wait_ge(s_read[n], SCRATCH_END)
            pe.wait_ge(s_wl, 1)
            pe.wait_ge(s_wh, 2)
            chunk(0, 0)
            chunk(1, 1)
            chunk(2, 0)
            chunk(3, 1)
            with pe.Fori(2, B // 2 - 1) as i:
                chunk(2 * i, 0)
                chunk(2 * i + 1, 1)
            chunk(B - 2, 0)
            chunk(B - 1, 1)
            chunk(B, 0)
            chunk(B + 1, 1)


def kernel(**inputs):
    import numpy as _np
    import concourse.bacc as _bacc
    from concourse import mybir as _mybir
    from concourse.bass_utils import run_bass_kernel_spmd as _run

    f = {k.split("_", 2)[2]: _np.asarray(v) for k, v in inputs.items() if k.startswith("L0_ffn")}
    a = {k.split("_", 2)[2]: _np.asarray(v) for k, v in inputs.items() if k.startswith("L0_attn")}

    inv_freq = 1.0 / 10000.0 ** (_np.arange(0, RD, 2, dtype=_np.float32) / RD)
    freqs = _np.outer(_np.arange(T, dtype=_np.float32), inv_freq)
    emb = _np.concatenate([freqs, freqs], -1)
    sign = _np.where(_np.arange(RD) < RD // 2, -1.0, 1.0)
    arrays = {
        "x": a["x"],
        "w_qkv": _np.concatenate([a["W_q"], a["W_kv"]], 1),
        "w_kvdec": _np.concatenate([a["W_kdec"], a["W_vdec"]], 1),
        "g_kv": a["g_kv"].reshape(KR, 1),
        "w_qdec": a["W_qdec"],
        "w_krope": a["W_krope"],
        "w_qrope": a["W_qrope"],
        "w_o": a["W_o"],
        "router": f["router_w"].T,
        "bias": f["correction_bias"],
        "gate": f["gate_w"].transpose(1, 0, 2).reshape(C, E * HE),
        "up": f["up_w"].transpose(1, 0, 2).reshape(C, E * HE),
        "down": f["down_w"].reshape(E * HE, C),
        "sgate": f["shared_gate_w"].T,
        "sup": f["shared_up_w"].T,
        "sdown": f["shared_down_w"].T,
        "cos": _np.cos(emb).astype(_np.float32),
        "sin": (_np.sin(emb) * sign).astype(_np.float32),
    }
    nc = _bacc.Bacc("TRN2", target_bir_lowering=False, num_devices=1)
    f32 = _mybir.dt.float32
    sent, args = {}, []
    for name, v in arrays.items():
        sent["in_" + name] = _np.ascontiguousarray(v)
        args.append(nc.dram_tensor("in_" + name, v.shape, f32, kind="ExternalInput").ap())
    args.append(nc.dram_tensor("out_0", (B, T, C), f32, kind="ExternalOutput").ap())
    args.append(nc.dram_tensor("x1_kept", (B, T, C), f32, kind="Internal").ap())
    args.append(nc.dram_tensor("x1t_kept", (B, C, T), f32, kind="Internal").ap())
    args.append(nc.dram_tensor("weights_kept", (B, P, NT * E), f32, kind="Internal").ap())
    mla_moe_kernel(nc, *args)
    r = _run(nc, [sent], core_ids=[0])
    return r.results[0]["out_0"]
```
